# Optimizing a Trainium2 kernel written in Bass

```python
import numpy as np
import jax
import jax.numpy as jnp

def _softmax(x, axis=-1):
    return jax.nn.softmax(x, axis=axis)

def _gelu(x):
    return jax.nn.gelu(x, approximate=True)

def _silu(x):
    return jax.nn.silu(x)

def _sigmoid(x):
    return jax.nn.sigmoid(x)

def _layernorm(x, axis=-1, eps=1e-05):
    m = jnp.mean(x, axis=axis, keepdims=True)
    v = jnp.var(x, axis=axis, keepdims=True)
    return (x - m) / jnp.sqrt(v + eps)

def _scatter_add(tgt, idx, src, axis=0):
    return tgt.at[idx].add(src)

def _segment_sum(src, seg, n):
    return jax.ops.segment_sum(src, seg, n)
kernel_name = 'mk_hybrid_d1_jaxref_r8_05723e'

def setup_inputs(seed: int=0):
    np.random.seed(seed)
    _w = jnp.asarray

    def _L0_attn_a_setup():
        import jax, jax.numpy as jnp
        import numpy as np
        B, S, HID = (2, 256, 256)
        H, HKV, D = (16, 4, 128)
        ROPE_BASE = 1000000.0
        EPS = 1e-05

        def _layernorm(x, g, b):
            mu = jnp.mean(x, axis=-1, keepdims=True)
            var = jnp.mean(jnp.square(x - mu), axis=-1, keepdims=True)
            return (x - mu) * jax.lax.rsqrt(var + EPS) * g + b

        def _rope_tables(seq_len, dim, base):
            inv_freq = 1.0 / base ** (jnp.arange(0, dim, 2, dtype=jnp.float32) / dim)
            t = jnp.arange(seq_len, dtype=jnp.float32)
            freqs = jnp.outer(t, inv_freq)
            cos = jnp.concatenate([jnp.cos(freqs), jnp.cos(freqs)], axis=-1)
            sin = jnp.concatenate([jnp.sin(freqs), jnp.sin(freqs)], axis=-1)
            return (cos, sin)

        def _rotate_half(x):
            x1, x2 = jnp.split(x, 2, axis=-1)
            return jnp.concatenate([-x2, x1], axis=-1)
        key = jax.random.key(seed)
        k1, k2, k3 = jax.random.split(key, 3)
        return {'x': jax.random.normal(k1, (B, S, HID), dtype=jnp.float32), 'w_qkv': jax.random.normal(k2, ((H + 2 * HKV) * D, HID), dtype=jnp.float32) * 0.02, 'w_o': jax.random.normal(k3, (HID, H * D), dtype=jnp.float32) * 0.02, 'qn_g': jnp.ones((D,), jnp.float32), 'qn_b': jnp.zeros((D,), jnp.float32), 'kn_g': jnp.ones((D,), jnp.float32), 'kn_b': jnp.zeros((D,), jnp.float32)}
    _L0_attn_a_in = _L0_attn_a_setup()

    def _L0_attn_b_setup():
        import jax, jax.numpy as jnp
        import numpy as np
        import math
        H = 256
        B = 4
        T = 256
        LAYERS = 24
        INDEX = 3
        EPS = 1e-05

        def _layer_norm(x, g, b):
            m = jnp.mean(x, axis=-1, keepdims=True)
            v = jnp.mean((x - m) ** 2, axis=-1, keepdims=True)
            return (x - m) * jax.lax.rsqrt(v + EPS) * g + b

        def _time_shift(x):
            return jnp.pad(x, ((0, 0), (1, 0), (0, 0)))[:, :-1, :]

        def _wkv_run(k, v, tm_first, tm_decay):
            C = k.shape[-1]
            aa = jnp.zeros((C,), k.dtype)
            bb = jnp.zeros((C,), k.dtype)
            pp = jnp.full((C,), -1e+38, k.dtype)
            ww = tm_first + k
            p = jnp.maximum(pp, ww)
            e1 = jnp.exp(pp - p)
            e2 = jnp.exp(ww - p)
            a = e1 * aa + e2 * v
            b = e1 * bb + e2
            return a / b
        key = jax.random.key(seed)
        ks = jax.random.split(key, 9)
        i = jnp.arange(H, dtype=jnp.float32)
        r01 = INDEX / (LAYERS - 1)
        r1pz = 1.0 - INDEX / LAYERS
        tm_decay = -5.0 + 8.0 * (i / (H - 1)) ** (0.7 + 1.3 * r01)
        zigzag = ((jnp.arange(H) + 1) % 3 - 1).astype(jnp.float32) * 0.5
        tm_first = jnp.float32(math.log(0.3)) + zigzag
        xr = i / H
        tm_mk = (xr ** r1pz)[None, None, :]
        tm_mv = tm_mk + 0.3 * r01
        tm_mr = (xr ** (0.5 * r1pz))[None, None, :]
        cm_mk = (xr ** r1pz)[None, None, :]
        cm_mr = (xr ** r1pz)[None, None, :]
        s = 1.0 / math.sqrt(H)
        s4 = 1.0 / math.sqrt(4 * H)
        Wk = jax.random.normal(ks[0], (H, H), jnp.float32) * s
        Wv = jax.random.normal(ks[1], (H, H), jnp.float32) * s
        Wr = jax.random.normal(ks[2], (H, H), jnp.float32) * s
        Wo = jax.random.normal(ks[3], (H, H), jnp.float32) * s
        Wkey = jax.random.normal(ks[4], (4 * H, H), jnp.float32) * s
        Wval = jax.random.normal(ks[5], (H, 4 * H), jnp.float32) * s4
        Wcr = jax.random.normal(ks[6], (H, H), jnp.float32) * s
        x = jax.random.normal(ks[7], (B, T, H), jnp.float32)
        return {'x': x, 'ln1_g': jnp.ones((H,), jnp.float32), 'ln1_b': jnp.zeros((H,), jnp.float32), 'ln2_g': jnp.ones((H,), jnp.float32), 'ln2_b': jnp.zeros((H,), jnp.float32), 'tm_decay': tm_decay, 'tm_first': tm_first, 'tm_mk': tm_mk, 'tm_mv': tm_mv, 'tm_mr': tm_mr, 'Wk': Wk, 'Wv': Wv, 'Wr': Wr, 'Wo': Wo, 'cm_mk': cm_mk, 'cm_mr': cm_mr, 'Wkey': Wkey, 'Wval': Wval, 'Wcr': Wcr}
    _L0_attn_b_in = _L0_attn_b_setup()

    def _L0_ffn_setup():
        import jax, jax.numpy as jnp
        import numpy as np
        DIM_IN = 256
        DIM_HIDDEN = 1024
        key = jax.random.key(seed)
        k_x, k_g, k_u, k_d = jax.random.split(key, 4)
        s_in = 1.0 / np.sqrt(DIM_IN)
        s_hid = 1.0 / np.sqrt(DIM_HIDDEN)
        x = jax.random.normal(k_x, (4, 256, DIM_IN), dtype=jnp.float32)
        w_gate = jax.random.uniform(k_g, (DIM_HIDDEN, DIM_IN), jnp.float32, -s_in, s_in)
        w_up = jax.random.uniform(k_u, (DIM_HIDDEN, DIM_IN), jnp.float32, -s_in, s_in)
        w_down = jax.random.uniform(k_d, (DIM_IN, DIM_HIDDEN), jnp.float32, -s_hid, s_hid)
        return {'x': x, 'w_gate': w_gate, 'w_up': w_up, 'w_down': w_down}
    _L0_ffn_in = _L0_ffn_setup()
    _d = {'L0_attn_a_x': _L0_attn_a_in['x'], 'L0_attn_a_w_qkv': _L0_attn_a_in['w_qkv'], 'L0_attn_a_w_o': _L0_attn_a_in['w_o'], 'L0_attn_a_qn_g': _L0_attn_a_in['qn_g'], 'L0_attn_a_qn_b': _L0_attn_a_in['qn_b'], 'L0_attn_a_kn_g': _L0_attn_a_in['kn_g'], 'L0_attn_a_kn_b': _L0_attn_a_in['kn_b'], 'L0_attn_b_ln1_g': _L0_attn_b_in['ln1_g'], 'L0_attn_b_ln1_b': _L0_attn_b_in['ln1_b'], 'L0_attn_b_ln2_g': _L0_attn_b_in['ln2_g'], 'L0_attn_b_ln2_b': _L0_attn_b_in['ln2_b'], 'L0_attn_b_tm_decay': _L0_attn_b_in['tm_decay'], 'L0_attn_b_tm_first': _L0_attn_b_in['tm_first'], 'L0_attn_b_tm_mk': _L0_attn_b_in['tm_mk'], 'L0_attn_b_tm_mv': _L0_attn_b_in['tm_mv'], 'L0_attn_b_tm_mr': _L0_attn_b_in['tm_mr'], 'L0_attn_b_Wk': _L0_attn_b_in['Wk'], 'L0_attn_b_Wv': _L0_attn_b_in['Wv'], 'L0_attn_b_Wr': _L0_attn_b_in['Wr'], 'L0_attn_b_Wo': _L0_attn_b_in['Wo'], 'L0_attn_b_cm_mk': _L0_attn_b_in['cm_mk'], 'L0_attn_b_cm_mr': _L0_attn_b_in['cm_mr'], 'L0_attn_b_Wkey': _L0_attn_b_in['Wkey'], 'L0_attn_b_Wval': _L0_attn_b_in['Wval'], 'L0_attn_b_Wcr': _L0_attn_b_in['Wcr'], 'L0_ffn_w_gate': _L0_ffn_in['w_gate'], 'L0_ffn_w_up': _L0_ffn_in['w_up'], 'L0_ffn_w_down': _L0_ffn_in['w_down']}
    _x0 = _d['L0_attn_a_x']
    _d['L0_attn_a_x'] = jax.random.normal(jax.random.fold_in(jax.random.key(seed), 1), (16, 256, 256), dtype=_x0.dtype)
    del _x0
    return _d

def reference(L0_attn_a_x, L0_attn_a_w_qkv, L0_attn_a_w_o, L0_attn_a_qn_g, L0_attn_a_qn_b, L0_attn_a_kn_g, L0_attn_a_kn_b, L0_attn_b_ln1_g, L0_attn_b_ln1_b, L0_attn_b_ln2_g, L0_attn_b_ln2_b, L0_attn_b_tm_decay, L0_attn_b_tm_first, L0_attn_b_tm_mk, L0_attn_b_tm_mv, L0_attn_b_tm_mr, L0_attn_b_Wk, L0_attn_b_Wv, L0_attn_b_Wr, L0_attn_b_Wo, L0_attn_b_cm_mk, L0_attn_b_cm_mr, L0_attn_b_Wkey, L0_attn_b_Wval, L0_attn_b_Wcr, L0_ffn_w_gate, L0_ffn_w_up, L0_ffn_w_down):

    def _L0_attn_a_ref(x, w_qkv, w_o, qn_g, qn_b, kn_g, kn_b):
        import jax, jax.numpy as jnp
        import numpy as np
        B, S, HID = (2, 256, 256)
        H, HKV, D = (16, 4, 128)
        ROPE_BASE = 1000000.0
        EPS = 1e-05

        def _layernorm(x, g, b):
            mu = jnp.mean(x, axis=-1, keepdims=True)
            var = jnp.mean(jnp.square(x - mu), axis=-1, keepdims=True)
            return (x - mu) * jax.lax.rsqrt(var + EPS) * g + b

        def _rope_tables(seq_len, dim, base):
            inv_freq = 1.0 / base ** (jnp.arange(0, dim, 2, dtype=jnp.float32) / dim)
            t = jnp.arange(seq_len, dtype=jnp.float32)
            freqs = jnp.outer(t, inv_freq)
            cos = jnp.concatenate([jnp.cos(freqs), jnp.cos(freqs)], axis=-1)
            sin = jnp.concatenate([jnp.sin(freqs), jnp.sin(freqs)], axis=-1)
            return (cos, sin)

        def _rotate_half(x):
            x1, x2 = jnp.split(x, 2, axis=-1)
            return jnp.concatenate([-x2, x1], axis=-1)
        b, s, _ = x.shape
        qkv = jnp.einsum('bsh,oh->bso', x, w_qkv)
        q, k, v = jnp.split(qkv, [H * D, (H + HKV) * D], axis=-1)
        q = q.reshape(b, s, H, D).transpose(0, 2, 1, 3)
        k = k.reshape(b, s, HKV, D).transpose(0, 2, 1, 3)
        v = v.reshape(b, s, HKV, D).transpose(0, 2, 1, 3)
        q = _layernorm(q, qn_g, qn_b)
        k = _layernorm(k, kn_g, kn_b)
        cos, sin = _rope_tables(s, D, ROPE_BASE)
        q = q * cos + _rotate_half(q) * sin
        k = k * cos + _rotate_half(k) * sin
        rep = H // HKV
        k = jnp.repeat(k, rep, axis=1)
        v = jnp.repeat(v, rep, axis=1)
        scores = jnp.einsum('bhqd,bhkd->bhqk', q, k) / jnp.sqrt(jnp.float32(D))
        causal = jnp.triu(jnp.ones((s, s), dtype=bool), k=1)
        scores = jnp.where(causal, -jnp.inf, scores)
        weights = jax.nn.softmax(scores, axis=-1)
        attn = jnp.einsum('bhqk,bhkd->bhqd', weights, v)
        attn = attn.transpose(0, 2, 1, 3).reshape(b, s, H * D)
        return jnp.einsum('bsd,od->bso', attn, w_o)

    def _L0_attn_b_ref(x, ln1_g, ln1_b, ln2_g, ln2_b, tm_decay, tm_first, tm_mk, tm_mv, tm_mr, Wk, Wv, Wr, Wo, cm_mk, cm_mr, Wkey, Wval, Wcr):
        import jax, jax.numpy as jnp
        import numpy as np
        import math
        H = 256
        B = 4
        T = 256
        LAYERS = 24
        INDEX = 3
        EPS = 1e-05

        def _layer_norm(x, g, b):
            m = jnp.mean(x, axis=-1, keepdims=True)
            v = jnp.mean((x - m) ** 2, axis=-1, keepdims=True)
            return (x - m) * jax.lax.rsqrt(v + EPS) * g + b

        def _time_shift(x):
            return jnp.pad(x, ((0, 0), (1, 0), (0, 0)))[:, :-1, :]

        def _wkv_run(k, v, tm_first, tm_decay):
            C = k.shape[-1]
            aa = jnp.zeros((C,), k.dtype)
            bb = jnp.zeros((C,), k.dtype)
            pp = jnp.full((C,), -1e+38, k.dtype)
            ww = tm_first + k
            p = jnp.maximum(pp, ww)
            e1 = jnp.exp(pp - p)
            e2 = jnp.exp(ww - p)
            a = e1 * aa + e2 * v
            b = e1 * bb + e2
            return a / b
        h = _layer_norm(x, ln1_g, ln1_b)
        hh = _time_shift(h)
        k = (h * tm_mk + hh * (1 - tm_mk)) @ Wk.T
        v = (h * tm_mv + hh * (1 - tm_mv)) @ Wv.T
        r = (h * tm_mr + hh * (1 - tm_mr)) @ Wr.T
        wkv = _wkv_run(k, v, tm_first, tm_decay)
        x = x + jax.nn.sigmoid(r) * wkv @ Wo.T
        h = _layer_norm(x, ln2_g, ln2_b)
        hh = _time_shift(h)
        kk = (h * cm_mk + hh * (1 - cm_mk)) @ Wkey.T
        kv = jax.nn.silu(kk) @ Wval.T
        sr = jax.nn.sigmoid((h * cm_mr + hh * (1 - cm_mr)) @ Wcr.T)
        x = x + sr * kv
        return x

    def _L0_ffn_ref(x, w_gate, w_up, w_down):
        import jax, jax.numpy as jnp
        import numpy as np
        DIM_IN = 256
        DIM_HIDDEN = 1024
        gate = jnp.einsum('bsd,hd->bsh', x, w_gate)
        up = jnp.einsum('bsd,hd->bsh', x, w_up)
        gated = jax.nn.silu(gate) * up
        return jnp.einsum('bsh,dh->bsd', gated, w_down)
    x = L0_attn_a_x
    x = x + _L0_attn_a_ref(_layernorm(x, axis=-1), L0_attn_a_w_qkv, L0_attn_a_w_o, L0_attn_a_qn_g, L0_attn_a_qn_b, L0_attn_a_kn_g, L0_attn_a_kn_b)
    x = x + _L0_ffn_ref(_layernorm(x, axis=-1), L0_ffn_w_gate, L0_ffn_w_up, L0_ffn_w_down)
    x = x + _L0_attn_b_ref(_layernorm(x, axis=-1), L0_attn_b_ln1_g, L0_attn_b_ln1_b, L0_attn_b_ln2_g, L0_attn_b_ln2_b, L0_attn_b_tm_decay, L0_attn_b_tm_first, L0_attn_b_tm_mk, L0_attn_b_tm_mv, L0_attn_b_tm_mr, L0_attn_b_Wk, L0_attn_b_Wv, L0_attn_b_Wr, L0_attn_b_Wo, L0_attn_b_cm_mk, L0_attn_b_cm_mr, L0_attn_b_Wkey, L0_attn_b_Wval, L0_attn_b_Wcr)
    x = x + _L0_ffn_ref(_layernorm(x, axis=-1), L0_ffn_w_gate, L0_ffn_w_up, L0_ffn_w_down)
    return x

_drawn_inputs = setup_inputs


def setup_inputs(seed=0):
    import zlib

    import numpy as np

    out = dict(_drawn_inputs(seed))
    spreads = {'L0_attn_a_qn_g': (1.0, 0.6),
     'L0_attn_a_qn_b': (0.0, 0.8),
     'L0_attn_a_kn_g': (1.0, 0.6),
     'L0_attn_a_kn_b': (0.0, 0.8),
     'L0_attn_b_ln1_g': (1.0, 0.2),
     'L0_attn_b_ln1_b': (0.0, 0.295),
     'L0_attn_b_ln2_g': (1.0, 0.548),
     'L0_attn_b_ln2_b': (0.0, 0.477)}
    factors = {}
    for name, (base, spread) in spreads.items():
        noise = np.random.default_rng([zlib.crc32(name.encode()), seed]).standard_normal(out[name].shape)
        drawn = base * np.exp(spread * noise) if base else spread * noise
        out[name] = jnp.asarray(drawn.astype(out[name].dtype))
    for name, factor in factors.items():
        out[name] = (out[name] * factor).astype(out[name].dtype)
    return out
```

```python
from contextlib import ExitStack

import concourse.bass as bass
from concourse import mybir

F32 = mybir.dt.float32
F32R = mybir.dt.float32r
BF16 = mybir.dt.bfloat16
ALU = mybir.AluOpType
ACT = mybir.ActivationFunctionType
AX = mybir.AxisListType

P = 128
NSEQ, SEQ, HID = 16, 256, 256
NB = SEQ // P
NK = HID // P
HEADS, KV, D = 16, 4, 128
REP = HEADS // KV
NG = KV
GW = (REP + 2) * D
QC = REP * D
FF = 1024
NF = FF // P
EPS = 1e-5
MASKED = -1e30
BANK = 512


def nth(per, i, k):
    value = i * per + k + 1
    return max(value, 1) if isinstance(value, int) else value


def products(pe, out, lhs, rhs, first, last):
    passes = ((0, 0), (0, 1), (1, 0))
    for n, (a, b) in enumerate(passes):
        mm = pe.matmul(out, lhs[a], rhs[b], start=first and n == 0, stop=last and n == 2, skip_group_check=True)
    return mm


def kernel_program(nc, x_in, w_group, w_out, qg, qb, kg, kb, cos_t, sin_t, ident_in, identb_in, mask_in,
                   w_tail, cols_in, out):
    ctx = ExitStack()
    with ctx:
        def sb(name, shape, dt=F32, c=ctx):
            return c.enter_context(nc.sbuf_tensor(name, shape, dt))

        def sem(name):
            return ctx.enter_context(nc.semaphore(name))

        x = sb("x", [P, NSEQ * NB, HID])
        ident = sb("ident", [P, P])
        banks = [ctx.enter_context(nc.psum_tensor(f"bank{n}", [P, BANK], F32)) for n in range(8)]
        x_loaded = [sem("x_first_loaded"), sem("x_rest_loaded")]
        const_loaded = sem("const_loaded")
        with ExitStack() as mem:
            attention(nc, lambda n, s, d=F32: sb(n, s, d, mem), sem, banks, x, ident, x_loaded, const_loaded,
                      x_in, w_group, w_out, qg, qb, kg, kb, cos_t, sin_t, ident_in, identb_in, mask_in)
        with ExitStack() as mem:
            tail(nc, lambda n, s, d=F32: sb(n, s, d, mem), sem, banks, x, ident, w_tail, cols_in)
        store(nc, sem, x, out)


def store(nc, sem, x, out):
    stored = sem("stored")
    with nc.Block() as block:
        @block.sync
        def _(sp):
            sp.dma_start(out.rearrange("s (b p) c -> p (s b) c", p=P), x[:, :, :]).then_inc(stored, 16)
            sp.wait_ge(stored, 16)


def attention(nc, sb, sem, banks, x, ident, x_loaded, const_loaded,
              x_in, w_group, w_out, qg, qb, kg, kb, cos_t, sin_t, ident_in, identb_in, mask_in):
    wg = [sb(f"wg_{p}", [P, NK, NG, GW], F32R) for p in ("hi", "lo")]
    wo = [sb(f"wo_{p}", [P, HEADS, HID], F32R) for p in ("hi", "lo")]
    identb = sb("identb", [P, P], BF16)
    mask = sb("mask", [P, P], BF16)
    cos = sb("cos", [P, NB, D])
    sin = sb("sin", [P, NB, D])
    gain = sb("gain", [P, 2, D])
    bias = sb("bias", [P, 2, D])
    tabA = sb("tabA", [P, 2, NB, D])
    tabB = sb("tabB", [P, 2, NB, D])
    tabC = sb("tabC", [P, 2, NB, D])
    xhat = sb("xhat", [P, NB, HID])
    ln_stats = sb("ln_stats", [P, NB, 6])
    ln_mv = sb("ln_mv", [P, NB, 2])
    ln_ve = sb("ln_ve", [P, NB])
    ln_rstd = sb("ln_rstd", [P, NB])
    spare = sb("spare", [P, 1])
    deps = sb("deps", [P, REP])
    half = sb("half", [P, 8])
    xT = [sb(f"xT_{p}", [P, NK, SEQ], F32R) for p in ("hi", "lo")]
    sq = sb("sq", [P, 3, QC])
    ssum = sb("ssum", [P, 3, REP])
    ve = sb("ve", [P, 3, REP])
    rstd = sb("rstd", [P, 3, REP])
    qn = sb("qn", [P, 3, QC])
    m1 = sb("m1", [P, 3, QC])
    m2 = sb("m2", [P, 3, QC])
    v = [sb(f"v_{p}", [P, NG, NB, D], F32R) for p in ("hi", "lo")]
    qT = [sb(f"qT_{p}", [P, 3, QC], F32R) for p in ("hi", "lo")]
    probs = sb("probs", [P, 3, BANK])
    negmax = sb("negmax", [P, 8])
    psum_ = sb("rowsum", [P, 8])
    rinv = sb("rinv", [P, 8])
    pT = [sb(f"pT_{p}", [P, 3, REP, P], F32R) for p in ("hi", "lo")]
    oT = [sb(f"oT_{p}", [P, NB, REP, P], F32R) for p in ("hi", "lo")]

    A = banks[0:2]
    T = banks[2:5]
    S = banks[5:7]
    W = banks[7]
    UA, US = 3, 3
    UT = 8 * NG + 1

    w_loaded = [sem(f"w_loaded{n}") for n in range(6)]
    w_hi, w_free = sem("w_hi"), sem("w_free")
    tab = sem("tab")
    const_made = sem("const_made")
    ln_s, ln_a = sem("ln_stats_made"), sem("ln_aggregated")
    ln_v, ln_r, ln_x = sem("ln_var_ready"), sem("ln_rstd_ready"), sem("xhat_ready")
    qkv_ready, sq_ready, var_ready = sem("qkv_ready"), sem("sq_ready"), sem("var_ready")
    rstd_ready, qn_ready, m1_ready, m2_ready = sem("rstd_ready"), sem("qn_ready"), sem("m1_ready"), sem("m2_ready")
    rot_ready = sem("rotated")
    v_hi, v_ready = sem("v_hi_ready"), sem("v_ready")
    t_ready, t_hi, t_split = sem("t_ready"), sem("t_hi"), sem("t_split")
    s_ready, s_max, s_exp = sem("s_ready"), sem("s_max_ready"), sem("s_exp_ready")
    r_ready, p_ready = sem("rinv_ready"), sem("probs_ready")
    wo_ready, wo_added = sem("wo_ready"), sem("wo_added")

    def skip(eng, s, i, g, use, n):
        if i == NSEQ and g > 1:
            return
        eng.wait_ge(s, nth(UT, i, 1 + use))
        eng.sem_inc(s, n)

    def real(i, g, lag):
        t = None if not isinstance(i, int) else NG * i + g - lag
        return (t is None or 0 <= t < NG * NSEQ), (g - lag) % NG

    def step(i, g, lag):
        return (i, g - lag)

    def more(i):
        return not isinstance(i, int) or i < NSEQ - 1

    def use_qk(g): return 8 * g
    def use_p(g): return 8 * g + 3
    def use_x(): return 8 * (NG - 1) + 6
    def use_o(g): return 8 * g + 6 + (g == NG - 1)

    SEQ0 = NSEQ

    def run(eng, body, before):
        before()
        for g in range(NG):
            body(0, g)
        with eng.Fori(1, NSEQ - 1) as i:
            for g in range(NG):
                body(i, g)
        for g in range(NG):
            body(NSEQ - 1, g)
        for g in range(3):
            body(NSEQ, g)

    STG = 6
    stage = [t[:, :, :].rearrange("p a b -> p (a b)")[:, n * GW:(n + 1) * GW] for t in (sq, qn, probs) for n in range(2)]
    pieces = [("g", k, g) for k in range(NK) for g in range(NG)] + [("o", h, min(3, HEADS - h)) for h in range(0, HEADS, 3)]

    def piece_ap(n, part):
        kind, a, b = pieces[n]
        return wg[part][:, a, b, :] if kind == "g" else wo[part][:, a:a + b, :].rearrange("p h n -> p (h n)")

    def piece_stage(n):
        kind, a, b = pieces[n]
        return stage[n % STG][:, 0:GW if kind == "g" else b * HID]

    csum = sb("csum", [P, REP + 1])
    cent = sem("centred")

    with nc.Block() as block:
        @block.sync
        def _(sp):
            xv = x_in.rearrange("s (b p) c -> p (s b) c", p=P)
            sp.dma_start(x[:, 0:NB, :], xv[:, 0:NB, :]).then_inc(x_loaded[0], 16)
            for n in range(len(pieces)):
                kind, a, b = pieces[n]
                if n == 2:
                    for dst, src in ((ident[:, :], ident_in), (identb[:, :], identb_in),
                                     (mask[:, :], mask_in),
                                     (cos[:, :, :], cos_t.rearrange("(b p) d -> p b d", p=P)),
                                     (sin[:, :, :], sin_t.rearrange("(b p) d -> p b d", p=P)),
                                     (gain[:, 0, :], qg.partition_broadcast(P)), (gain[:, 1, :], kg.partition_broadcast(P)),
                                     (bias[:, 0, :], qb.partition_broadcast(P)), (bias[:, 1, :], kb.partition_broadcast(P))):
                        sp.dma_start(dst, src).then_inc(const_loaded, 16)
                if n >= STG:
                    sp.wait_ge(w_free, n - STG + 1)
                src = w_group[a, b] if kind == "g" else w_out[:, a:a + b, :].rearrange("p h n -> p (h n)")
                sp.dma_start(piece_stage(n), src).then_inc(w_loaded[n % STG], 16)
            sp.dma_start(x[:, NB:, :], xv[:, NB:, :]).then_inc(x_loaded[1], 16)

        @block.tensor
        def _(pe):
            def begin():
                for s in (qkv_ready, t_ready, s_ready, wo_ready):
                    pe.sem_inc(s, 1)
                pe.wait_ge(const_loaded, 9 * 16)
                turn_x(0)

            def turn_x(i):
                pe.wait_ge(ln_x, nth(1, i, 1))
                for k in range(NK):
                    for b in range(NB):
                        mm = pe.transpose(T[xbank][:, (k * NB + b) * P:(k * NB + b + 1) * P],
                                          xhat[:, b, k * P:(k + 1) * P], ident[:, :])
                mm.then_inc(t_ready, 1)

            xbank = use_x() % 3

            def body(i, g):
                def project(u):
                    bank = A[(UA * g + u) % 2]
                    pe.wait_ge(qn_ready, nth(UA * NG, i, UA * g + u - 1))
                    if g == 0 and u == 0:
                        pe.wait_ge(t_split, nth(UT, i, 1))
                    if not isinstance(i, int) or i == 0:
                        if u == 0 and isinstance(i, int):
                            pe.wait_ge(w_free, 2 * NG)
                    for b in ((u,) if u < 2 else (0, 1)):
                        for k in range(NK):
                            cols = slice(0, QC) if u < 2 else slice(QC, GW)
                            o = bank[:, :] if u < 2 else bank[:, b * 2 * D:(b + 1) * 2 * D]
                            mm = products(pe, o, [w[:, k, b * P:(b + 1) * P] for w in xT],
                                          [w[:, k, g, cols] for w in wg], k == 0, k == NK - 1)
                    mm.then_inc(qkv_ready, 1)

                def turn_qk():
                    ok, _ = real(i, g, 1)
                    if not ok:
                        return skip(pe, t_ready, i, g, use_qk(g), 3)
                    for u in range(3):
                        use = use_qk(g) + u
                        pe.wait_ge(rot_ready, nth(UA * NG, i, UA * (g - 1) + u + 1))
                        pe.wait_ge(t_split, nth(UT, i, 1 + use - 2))
                        for h in range(REP if u < 2 else NB):
                            o = T[use % 3][:, h * P:(h + 1) * P]
                            c = tabC[:, 0, u, :] if u < 2 else tabC[:, 1, h, :]
                            for n, src in enumerate((m1[:, u, h * D:(h + 1) * D], c)):
                                mm = pe.matmul(o, src, ident[:, :], is_transpose=True, start=n == 0, stop=n == 1,
                                               skip_group_check=True)
                        mm.then_inc(t_ready, 1)

                def turn_probs():
                    ok, _ = real(i, g, 2)
                    if not ok:
                        return skip(pe, t_ready, i, g, use_p(g), 3)
                    pe.wait_ge(p_ready, nth(NG, i, g - 2 + 1))
                    for u in range(3):
                        use = use_p(g) + u
                        pe.wait_ge(t_split, nth(UT, i, 1 + use - 2))
                        for h in range(REP):
                            src = (probs[:, 0, h * P:(h + 1) * P] if u == 0 else
                                   probs[:, 1 + h // 2, (h % 2) * SEQ + (u - 1) * P:(h % 2) * SEQ + u * P])
                            mm = pe.transpose(T[use % 3][:, h * P:(h + 1) * P], src, ident[:, :])
                        mm.then_inc(t_ready, 1)

                def scores(u):
                    if not real(i, g, 1)[0]:
                        return
                    if u == 0:
                        pe.wait_ge(t_split, nth(UT, i, 1 + use_qk(g) + 3))
                    bank = S[(US * (g - 1) + u) % 2]
                    pe.wait_ge(s_exp, nth(US * NG, i, US * (g - 1) + u - 1))
                    keys, heads = (P, range(REP)) if u == 0 else (SEQ, range(2 * u - 2, 2 * u))
                    for n, h in enumerate(heads):
                        o = bank[:, n * keys:(n + 1) * keys]
                        products(pe, o, [w[:, min(u, 1), h * P:(h + 1) * P] for w in qT],
                                 [w[:, 2, 0:keys] for w in qT], True, False)
                        mm = pe.matmul(o[:, keys - P:keys], identb[:, :], mask[:, :], start=False, stop=True,
                                       skip_group_check=True)
                    mm.then_inc(s_ready, 1)

                def sums():
                    ok, gv = real(i, g, 2)
                    if not ok:
                        return skip(pe, t_ready, i, g, use_o(g), 2)
                    pe.wait_ge(t_split, nth(UT, i, 1 + use_p(g) + 3))
                    pe.wait_ge(v_ready, nth(NG, i, g - 2 + 1))
                    for b in range(NB):
                        use = use_o(g) + b
                        pe.wait_ge(t_split, nth(UT, i, 1 + use - 2))
                        for kb_ in range(b + 1):
                            mm = products(pe, T[use % 3][:, :], [w[:, gv, kb_, :] for w in v],
                                          [w[:, b + kb_, :, :].rearrange("p h q -> p (h q)") for w in pT],
                                          kb_ == 0, kb_ == b)
                        mm.then_inc(t_ready, 1)

                def project_out():
                    ok, go = real(i, g, 3)
                    if not ok:
                        return
                    pe.wait_ge(t_split, nth(UT, i, 1 + (use_o(g - 1) + 2 if g else use_o(NG - 1) + 2 - UT)))
                    if go == 0:
                        if isinstance(i, int) and i == 0:
                            pe.wait_ge(w_free, len(pieces))
                        pe.wait_ge(wo_added, nth(1, i, 0 if g == 3 else -1))
                    for b in range(NB):
                        for h in range(REP):
                            mm = products(pe, W[:, b * HID:(b + 1) * HID], [w[:, b, h, :] for w in oT],
                                          [w[:, go * REP + h, :] for w in wo],
                                          go == 0 and b == 0 and h == 0, go == NG - 1 and h == REP - 1)
                    if go == NG - 1:
                        mm.then_inc(wo_ready, 1)

                new = not isinstance(i, int) or i < NSEQ
                if new:
                    project(0)
                    project(1)
                turn_qk()
                project_out()
                turn_probs()
                scores(0)
                scores(1)
                if new:
                    project(2)
                if g == NG - 1:
                    turn_x_next(i)
                scores(2)
                sums()

            def turn_x_next(i):
                pe.wait_ge(t_split, nth(UT, i, 1 + use_x() - 2))
                turn_x(i + 1 if more(i) else i)

            run(pe, body, begin)

        @block.scalar
        def _(act):
            def begin():
                for s in (sq_ready, qn_ready, v_hi, t_hi, s_exp):
                    act.sem_inc(s, 1)
                for n in range(len(pieces)):
                    act.wait_ge(w_loaded[n % STG], 16 * (n // STG + 1))
                    if pieces[n][0] == "g":
                        act.wait_ge(cent, 2 * (n + 1))
                    act.copy(piece_ap(n, 0), piece_stage(n)).then_inc(w_hi, 1)
                    if n == 2 * NG - 1:
                        split_hi(0, 0, xT[0][:, :, :].rearrange("p k n -> p (k n)"), xb)

            xb = use_x() % 3

            def split_hi(i, count, dst, bank, width=BANK):
                act.wait_ge(t_ready, nth(UT, i, count + 1))
                act.copy(dst, T[bank][:, 0:width]).then_inc(t_hi, 1)

            def body(i, g):
                def square(u):
                    act.wait_ge(qkv_ready, nth(UA * NG, i, UA * g + u + 1))
                    act.wait_ge(rstd_ready, nth(UA * NG, i, UA * (g - 1) + u + 1))
                    if isinstance(i, int) and i == 0 and g == 0 and u == 0:
                        act.wait_ge(w_free, len(pieces))
                    bank = A[(UA * g + u) % 2]
                    for h in range(REP if u < 2 else NB):
                        at = h * D if u < 2 else h * 2 * D
                        a = act.activation(sq[:, u, h * D:(h + 1) * D], bank[:, at:at + D], ACT.Square,
                                           accum_out=ssum[:, u, h:h + 1])
                    a.then_inc(sq_ready, 1)
                    if u == 2:
                        kv = bank[:, :].rearrange("p (b s d) -> p b s d", b=NB, s=2)
                        act.wait_ge(t_ready, nth(UT, i, 1 + 8 * g - 8))
                        act.copy(v[0][:, g, :, :], kv[:, :, 1, :]).then_inc(v_hi, 1)

                def normalise(u):
                    if u == 2:
                        act.wait_ge(v_ready, nth(NG, i, g + 1))
                    act.wait_ge(rstd_ready, nth(UA * NG, i, UA * g + u + 1))
                    act.wait_ge(rot_ready, nth(UA * NG, i, UA * (g - 1) + u + 1))
                    bank = A[(UA * g + u) % 2]
                    for h in range(REP if u < 2 else NB):
                        at = h * D if u < 2 else h * 2 * D
                        a = act.activation(qn[:, u, h * D:(h + 1) * D], bank[:, at:at + D], ACT.Copy,
                                           scale=rstd[:, u, h:h + 1])
                    a.then_inc(qn_ready, 1)

                def hi_qk():
                    if not real(i, g, 1)[0]:
                        return skip(act, t_hi, i, g, use_qk(g), 3)
                    act.wait_ge(s_ready, nth(US * NG, i, US * (g - 1)))
                    for u in range(3):
                        w = QC if u < 2 else NB * P
                        split_hi(i, 1 + use_qk(g) + u, qT[0][:, u, 0:w], (use_qk(g) + u) % 3, w)

                def hi_probs():
                    if not real(i, g, 2)[0]:
                        return skip(act, t_hi, i, g, use_p(g), 3)
                    for u in range(3):
                        split_hi(i, 1 + use_p(g) + u, pT[0][:, u, :, :].rearrange("p h q -> p (h q)"), (use_p(g) + u) % 3)

                def exps(u):
                    if not real(i, g, 1)[0]:
                        return
                    if u == 0:
                        act.wait_ge(t_ready, nth(UT, i, 1 + use_p(g) + 3))
                    act.wait_ge(s_max, nth(US * NG, i, US * (g - 1) + u + 1))
                    bank = S[(US * (g - 1) + u) % 2]
                    keys, n = (P, REP) if u == 0 else (SEQ, 2)
                    for h in range(n):
                        r = h if u == 0 else 2 + 2 * u + h
                        a = act.activation(probs[:, u, h * keys:(h + 1) * keys], bank[:, h * keys:(h + 1) * keys],
                                           ACT.Exp, bias=negmax[:, r:r + 1], accum_out=psum_[:, r:r + 1])
                    a.then_inc(s_exp, 1)

                def hi_o():
                    if not real(i, g, 2)[0]:
                        return skip(act, t_hi, i, g, use_o(g), 2)
                    for b in range(NB):
                        split_hi(i, 1 + use_o(g) + b, oT[0][:, b, :, :].rearrange("p h q -> p (h q)"), (use_o(g) + b) % 3)

                new = not isinstance(i, int) or i < NSEQ
                if new:
                    square(0)
                    square(1)
                hi_qk()
                if new:
                    normalise(0)
                    normalise(1)
                hi_probs()
                exps(0)
                exps(1)
                if new:
                    square(2)
                if g == NG - 1:
                    split_hi(i, 1 + use_x(), xT[0][:, :, :].rearrange("p k n -> p (k n)"), xb)
                exps(2)
                if new:
                    normalise(2)
                hi_o()

            run(act, body, begin)

        @block.gpsimd
        def _(pool):
            def begin():
                for s in (rstd_ready, m2_ready, ln_r, var_ready):
                    pool.sem_inc(s, 1)
                pool.memset(half[:, :], -0.5).then_inc(const_made, 1)
                pool.memset(deps[:, :], D * EPS).then_inc(const_made, 1)
                pool.wait_ge(const_made, 2)
                ln_power(0)

            def ln_power(i):
                pool.wait_ge(ln_v, nth(1, i, 1))
                pool.tensor_tensor(ln_rstd[:, :], ln_ve[:, :], half[:, 0:NB], ALU.pow).then_inc(ln_r, 1)

            def body(i, g):
                new = not isinstance(i, int) or i < NSEQ

                def power(u):
                    n = REP if u < 2 else NB
                    pool.wait_ge(sq_ready, nth(UA * NG, i, UA * g + u + 1))
                    pool.tensor_tensor(ve[:, u, 0:n], ssum[:, u, 0:n], deps[:, 0:n], ALU.add).then_inc(var_ready, 1)
                    pool.wait_ge(var_ready, nth(UA * NG, i, UA * g + u + 1))
                    pool.tensor_tensor(rstd[:, u, 0:n], ve[:, u, 0:n], half[:, 0:n], ALU.pow).then_inc(rstd_ready, 1)

                def second(u):
                    pool.wait_ge(qn_ready, nth(UA * NG, i, UA * g + u + 1))
                    pool.wait_ge(rot_ready, nth(UA * NG, i, UA * (g - 1) + u + 1))
                    n = REP if u < 2 else NB
                    q = qn[:, u, 0:n * D].rearrange("p (h s d) -> p h s d", s=2, d=D // 2)
                    o = m2[:, u, 0:n * D].rearrange("p (h s d) -> p h s d", s=2, d=D // 2)
                    if u < 2:
                        b = tabB[:, 0, u:u + 1, :].rearrange("p o (s d) -> p o s d", s=2).broadcast_to([P, n, 2, D // 2])
                    else:
                        b = tabB[:, 1, :, :].rearrange("p b (s d) -> p b s d", s=2)
                    pool.tensor_tensor(o[:, :, ::-1, :], q, b, ALU.mult).then_inc(m2_ready, 1)

                if new:
                    power(0)
                    power(1)
                    if g == 0 and isinstance(i, int):
                        pool.wait_ge(tab, 6)
                    second(0)
                    second(1)
                    power(2)
                    second(2)
                    if g == 2:
                        if more(i):
                            ln_power(i + 1)

            run(pool, body, begin)

        @block.vector
        def _(dve):
            def begin():
                for s in (m1_ready, rot_ready, v_ready, t_split, s_max, r_ready, p_ready, wo_added, ln_s,
                          ln_a, ln_v, ln_x):
                    dve.sem_inc(s, 1)
                ln_stat(0)
                ln_apply(0)
                for n in range(len(pieces)):
                    dve.wait_ge(w_loaded[n % STG], 16 * (n // STG + 1))
                    st = piece_stage(n)
                    if pieces[n][0] == "g":
                        heads = st.rearrange("p (h d) -> p h d", d=D)[:, 0:REP + 1, :]
                        dve.tensor_reduce(csum[:, :], heads, AX.X, ALU.add).then_inc(cent, 1)
                        dve.wait_ge(cent, 2 * n + 1)
                        dve.scalar_tensor_tensor(heads, csum[:, :].unsqueeze(2).broadcast_to([P, REP + 1, D]), -1.0 / D,
                                                 heads, ALU.mult, ALU.add).then_inc(cent, 1)
                    dve.wait_ge(w_hi, n + 1)
                    dve.tensor_tensor(piece_ap(n, 1), st, piece_ap(n, 0).bitcast(F32), ALU.subtract).then_inc(w_free, 1)
                    if n == 2 * NG - 1:
                        split_lo(0, 0, xT[0][:, :, :].rearrange("p k n -> p (k n)"),
                                 xT[1][:, :, :].rearrange("p k n -> p (k n)"), use_x() % 3)
                        tables()

            def tables():
                dve.wait_ge(const_loaded, 9 * 16)
                for w, s in ((0, 1.0), (1, float(D) ** 0.5)):
                    g = gain[:, w:w + 1, :].broadcast_to([P, NB, D])
                    b = bias[:, w:w + 1, :].broadcast_to([P, NB, D])
                    dve.scalar_tensor_tensor(tabA[:, w, :, :], cos[:, :, :], s, g, ALU.mult, ALU.mult).then_inc(tab, 1)
                    dve.scalar_tensor_tensor(tabB[:, w, :, :], sin[:, :, :], s, g, ALU.mult, ALU.mult).then_inc(tab, 1)
                    dve.scalar_tensor_tensor(tabC[:, w, :, :], cos[:, :, :], s * float(D) ** -0.5, b, ALU.mult, ALU.mult).then_inc(tab, 1)
                for w, s in ((0, float(D) ** -0.5), (1, 1.0)):
                    b = bias[:, w:w + 1, :].broadcast_to([P, NB, D])
                    if w:
                        dve.wait_ge(tab, 8)
                    dve.scalar_tensor_tensor(m1[:, 0, 0:NB * D].rearrange("p (b d) -> p b d", b=NB), sin[:, :, :], s, b,
                                             ALU.mult, ALU.mult).then_inc(tab, 1)
                    dve.wait_ge(tab, 7 + 2 * w)
                    for half_ in range(2):
                        lo, hi = half_ * D // 2, (1 - half_) * D // 2
                        c = tabC[:, w, :, lo:lo + D // 2]
                        i_ = dve.tensor_tensor(c, c, m1[:, 0, 0:NB * D].rearrange("p (b d) -> p b d", b=NB)[:, :, hi:hi + D // 2],
                                               ALU.add)
                    i_.then_inc(tab, 1)
                dve.wait_ge(tab, 10)

            def ln_stat(i):
                if isinstance(i, int) and i < 2:
                    dve.wait_ge(x_loaded[i], 16)
                for b in range(NB):
                    xb = x[:, bass.ds(i * NB + b, 1), :].rearrange("p o c -> p (o c)")
                    a = dve.bn_stats(ln_stats[:, b, :], xb)
                a.then_inc(ln_s, 1)
                dve.wait_ge(ln_s, nth(1, i, 1))
                dve.memset(spare[:, :], 0.0)
                for b in range(NB):
                    a = dve.bn_aggr(ln_mv[:, b, :], ln_stats[:, b, :])
                a.then_inc(ln_a, 1)
                dve.wait_ge(ln_a, nth(1, i, 1))
                dve.tensor_scalar(ln_ve[:, :], ln_mv[:, :, 1], EPS, None, ALU.add).then_inc(ln_v, 1)

            def ln_apply(i):
                dve.wait_ge(ln_r, nth(1, i, 1))
                for b in range(NB):
                    xb = x[:, bass.ds(i * NB + b, 1), :].rearrange("p o c -> p (o c)")
                    a = dve.tensor_scalar(xhat[:, b, :], xb, ln_mv[:, b, 0:1], ln_rstd[:, b:b + 1], ALU.subtract, ALU.mult)
                a.then_inc(ln_x, 1)

            def split_lo(i, count, hi, lo, bank, width=BANK):
                dve.wait_ge(t_hi, nth(UT, i, count + 1))
                dve.tensor_tensor(lo, T[bank][:, 0:width], hi.bitcast(F32), ALU.subtract).then_inc(t_split, 1)

            def body(i, g):
                new = not isinstance(i, int) or i < NSEQ

                def first(u):
                    dve.wait_ge(qn_ready, nth(UA * NG, i, UA * g + u + 1))
                    dve.wait_ge(t_ready, nth(UT, i, 1 + use_qk(g) - 8 + u + 1 - (g == 0)))
                    n = REP if u < 2 else NB
                    a = tabA[:, 0, u:u + 1, :].broadcast_to([P, n, D]) if u < 2 else tabA[:, 1, :, :]
                    dve.tensor_tensor(m1[:, u, 0:n * D].rearrange("p (h d) -> p h d", d=D),
                                      qn[:, u, 0:n * D].rearrange("p (h d) -> p h d", d=D), a, ALU.mult).then_inc(m1_ready, 1)

                def rotate(u):
                    dve.wait_ge(m1_ready, nth(UA * NG, i, UA * g + u + 1))
                    dve.wait_ge(m2_ready, nth(UA * NG, i, UA * g + u + 1))
                    n = QC if u < 2 else NB * D
                    dve.tensor_tensor(m1[:, u, 0:n], m1[:, u, 0:n], m2[:, u, 0:n], ALU.add).then_inc(rot_ready, 1)

                def lo_v():
                    dve.wait_ge(v_hi, nth(NG, i, g + 1))
                    kv = A[(UA * g + 2) % 2][:, :].rearrange("p (b s d) -> p b s d", b=NB, s=2)
                    dve.tensor_tensor(v[1][:, g, :, :], kv[:, :, 1, :], v[0][:, g, :, :].bitcast(F32),
                                      ALU.subtract).then_inc(v_ready, 1)

                def lo_qk():
                    if not real(i, g, 1)[0]:
                        return skip(dve, t_split, i, g, use_qk(g), 3)
                    for u in range(3):
                        w = QC if u < 2 else NB * P
                        split_lo(i, 1 + use_qk(g) + u, qT[0][:, u, 0:w], qT[1][:, u, 0:w], (use_qk(g) + u) % 3, w)

                def lo_probs():
                    if not real(i, g, 2)[0]:
                        return skip(dve, t_split, i, g, use_p(g), 3)
                    for u in range(3):
                        split_lo(i, 1 + use_p(g) + u, pT[0][:, u, :, :].rearrange("p h q -> p (h q)"),
                                 pT[1][:, u, :, :].rearrange("p h q -> p (h q)"), (use_p(g) + u) % 3)

                def lo_o():
                    if not real(i, g, 2)[0]:
                        return skip(dve, t_split, i, g, use_o(g), 2)
                    for b in range(NB):
                        split_lo(i, 1 + use_o(g) + b, oT[0][:, b, :, :].rearrange("p h q -> p (h q)"),
                                 oT[1][:, b, :, :].rearrange("p h q -> p (h q)"), (use_o(g) + b) % 3)

                def maxima(u):
                    if not real(i, g, 1)[0]:
                        return
                    dve.wait_ge(s_ready, nth(US * NG, i, US * (g - 1) + u + 1))
                    dve.wait_ge(s_exp, nth(US * NG, i, US * (g - 2) + u + 1))
                    n = REP if u == 0 else 2
                    r = 0 if u == 0 else 2 + 2 * u
                    dve.tensor_reduce(negmax[:, r:r + n], S[(US * (g - 1) + u) % 2][:, :].rearrange("p (h k) -> p h k", h=n),
                                      AX.X, ALU.max, negate=True).then_inc(s_max, 1)

                def norm():
                    if not real(i, g, 2)[0]:
                        return
                    dve.wait_ge(s_exp, nth(US * NG, i, US * (g - 1)))
                    dve.reciprocal(rinv[:, :], psum_[:, :]).then_inc(r_ready, 1)
                    dve.wait_ge(r_ready, nth(NG, i, g - 1))
                    for u in range(3):
                        n = REP if u == 0 else 2
                        r = 0 if u == 0 else 2 + 2 * u
                        pr = probs[:, u, :].rearrange("p (h k) -> p h k", h=n)
                        a = dve.tensor_tensor(pr, pr, rinv[:, r:r + n].unsqueeze(2).broadcast_to([P, n, BANK // n]), ALU.mult)
                    a.then_inc(p_ready, 1)

                norm()
                lo_qk()
                if new:
                    first(0)
                    first(1)
                lo_probs()
                maxima(0)
                maxima(1)
                if new:
                    rotate(0)
                    rotate(1)
                    lo_v()
                if g == NG - 1:
                    split_lo(i, 1 + use_x(), xT[0][:, :, :].rearrange("p k n -> p (k n)"),
                             xT[1][:, :, :].rearrange("p k n -> p (k n)"), use_x() % 3)
                maxima(2)
                if new:
                    first(2)
                lo_o()
                if new:
                    rotate(2)
                if g == 1 and more(i):
                    ln_stat(i + 1)
                if g == 2:
                    if more(i):
                        ln_apply(i + 1)
                    if not isinstance(i, int) or i >= 1:
                        dve.wait_ge(wo_ready, nth(1, i, 0))
                        xb = x[:, bass.ds((i - 1) * NB, NB), :].rearrange("p b c -> p (b c)")
                        dve.tensor_tensor(xb, W[:, :], xb, ALU.add).then_inc(wo_added, 1)

            run(dve, body, begin)


PW = 2 * BANK
NP2 = 13
PP0 = -1e38
LAST = 3
LG1, LB1, LG2, LB2, FIRST, MK, MV, MR, CK, CR, NCOL = range(11)


def norm_state(sb, sem, name):
    return {
        "stats": sb(f"{name}_stats", [P, NB, 6]), "mv": sb(f"{name}_mv", [P, NB, 2]), "ve": sb(f"{name}_ve", [P, NB]),
        "rstd": sb(f"{name}_rstd", [P, NB]), "spare": sb(f"{name}_spare", [P, 1]),
        "stats_made": sem(f"{name}_stats_made"), "aggregated": sem(f"{name}_aggregated"),
        "var_ready": sem(f"{name}_var_ready"), "rstd_ready": sem(f"{name}_rstd_ready"), "normed": sem(f"{name}_normed"),
    }


def ffn_state(sb, sem, n, banks):
    state = {
        "acc": banks[0], "G": banks[1:3], "norm": norm_state(sb, sem, f"f{n}"), "xhat": sb(f"f{n}_xhat", [P, NB, HID]),
        "xT": [sb(f"f{n}_xT_{p}", [P, NK, SEQ], F32R) for p in ("hi", "lo")],
        "h": sb(f"f{n}_h", [P, 2, SEQ]),
        "hs": [sb(f"f{n}_h_{p}", [P, 2, SEQ], F32R) for p in ("hi", "lo")],
    }
    for name in ("x_turned", "x_hi", "x_split", "added", "gate_up", "tanh", "gated", "h_ready", "h_hi", "h_split", "down"):
        state[name if name not in ("tanh", "x_hi", "h_hi") else name + "_ready"] = sem(f"f{n}_{name}")
    return state


def tail(nc, sb, sem, banks, x, ident, w_tail, cols_in):
    wt = [sb(f"wt_{p}", [P, NP2, PW], F32R) for p in ("hi", "lo")]
    flat = [w[:, :, :].rearrange("p a b -> p (a b)") for w in wt]

    def weights(piece, chunks, width, skip=0):
        at = piece * PW + skip
        return [w[:, at:at + chunks * width].rearrange("p (c n) -> p c n", c=chunks) for w in flat]

    w_gate, w_up, w_down = weights(0, NK, FF), weights(2, NK, FF), weights(4, NF, HID)
    w_key, w_val = weights(6, NK, FF), weights(8, NF, HID)
    w_proj = [weights(10, NK, HID), weights(10, NK, HID, BANK), weights(11, NK, HID)]
    w_ob, w_cr = weights(11, NK, HID, BANK), weights(12, NK, HID)

    def ranges(n):
        if n == 11:
            return [(0, BANK, 1.0), (BANK, PW, 0.5)]
        return [(0, BANK if n == 12 else PW, {4: 0.5, 5: 0.5, 8: 0.25, 9: 0.25}.get(n, 1.0))]

    cols = sb("cols", [P, NCOL, NK])
    half = sb("half2", [P, NB])
    f1, f2 = ffn_state(sb, sem, 1, banks[0:3]), ffn_state(sb, sem, 2, banks[3:6])
    R = banks[6:8]
    rn = norm_state(sb, sem, "r")
    yh = sb("r_yhat", [P, NB, HID])
    diff = yh[:, :, :]
    hT = sb("r_hT", [P, NK, SEQ + 1])
    mixf = sb("r_mix", [P, 2, NK, SEQ])
    mixs = [[sb(f"r_mix{m}_{p}", [P, NK, SEQ], F32R) for p in ("hi", "lo")] for m in range(3)]
    er = sb("r_e2_rinv", [P, 2, NK, SEQ])
    e2, ri = er[:, 0, :, :], er[:, 1, :, :]
    yt = sb("r_y_th", [P, 2, NB, HID])
    y, th = yt[:, 0, :, :], yt[:, 1, :, :]
    ss = [sb(f"r_s_{p}", [P, NF, SEQ], F32R) for p in ("hi", "lo")]
    stage = [t[:, :, :, :].rearrange("p a b c -> p (a b c)") for t in (mixf, er, yt)]
    ST = len(stage)

    names = ("turned hT diffd mix mix_hi mix_split proj first floored exped recip av wkv rtanh o o_hi o_split oproj "
             "y_added xy_added key ktanh s s_hi s_split cr ctanh val u x_added").split()
    (turned, h_ready, diffed, mixed, mix_hi, mix_split, proj, first, floored, exped, recip, av, wkv, rtanh, o_ready, o_hi,
     o_split, oproj, y_added, xy_added, key, ktanh, s_ready, s_hi, s_split, cr, ctanh, val, u_ready, x_added) = (
        sem(f"r_{n}") for n in names)
    w_loaded = [sem(f"w2_loaded{n}") for n in range(ST)]
    w_hi, w_free, cols_loaded, made, made_h = (sem(n) for n in ("w2_hi", "w2_free", "cols_loaded", "made2", "made_h"))

    USES = 12
    READ = [(h_ready, 2, 1), (first, 1, 1), (av, 1, 1), (rtanh, 1, 1), (y_added, 1, 1), (h_ready, 2, 2),
            (s_ready, 4, 1), (s_ready, 4, 2), (s_ready, 4, 3), (s_ready, 4, 4), (ctanh, 1, 1), (u_ready, 1, 1)]

    def rows(j, b, n=1):
        return x[:, bass.ds(j * NB + b, n), :].rearrange("p o c -> p (o c)")

    def run(eng, ffn_prep, ffn_block, ffn_end, rwkv):
        def body(i):
            def on(lag):
                return not isinstance(i, int) or 0 <= i - lag < NSEQ

            def r(n):
                if on(2):
                    rwkv(i - 2, n)

            def prep1(part):
                if on(0):
                    ffn_prep(f1, i, part)
            if on(LAST):
                ffn_prep(f2, i - LAST, 0)
            r(0)
            if on(LAST):
                ffn_prep(f2, i - LAST, 1)
            for t in range(NF + 2):
                if on(1):
                    ffn_block(f1, i - 1, t)
                r(1 + 2 * t)
                if on(LAST):
                    ffn_block(f2, i - LAST, t)
                r(2 + 2 * t)
                if t == NF - 2:
                    prep1(0)
            if on(1):
                ffn_end(f1, i - 1)
            if on(LAST):
                ffn_end(f2, i - LAST)
            prep1(1)
        for i in range(LAST + 1):
            body(i)
        with eng.Fori(LAST + 1, NSEQ) as i:
            body(i)
        for i in range(NSEQ, NSEQ + LAST):
            body(i)

    with nc.Block() as block:
        @block.sync
        def _(sp):
            sp.dma_start(cols[:, :, :], cols_in).then_inc(cols_loaded, 16)
            for n in range(NP2):
                if n >= ST:
                    sp.wait_ge(w_free, n - ST + 1)
                width = ranges(n)[-1][1]
                sp.dma_start(stage[n % ST][:, 0:width], w_tail[:, n, 0:width]).then_inc(w_loaded[n % ST], 16)

        @block.tensor
        def _(pe):
            for s in (turned, proj, oproj, key, cr, val, *(f[n] for f in (f1, f2) for n in ("x_turned", "gate_up", "down"))):
                pe.sem_inc(s, 1)

            def turn(src, bank):
                for k in range(NK):
                    for b in range(NB):
                        mm = pe.transpose(bank[:, (k * NB + b) * P:(k * NB + b + 1) * P],
                                          src[:, b, k * P:(k + 1) * P], ident[:, :])
                return mm

            def ffn_prep(f, j, part):
                if part == 0:
                    return
                pe.wait_ge(f["norm"]["normed"], nth(1, j, 1))
                pe.wait_ge(f["added"], nth(1, j, 0))
                turn(f["xhat"], f["acc"]).then_inc(f["x_turned"], 1)

            def ffn_block(f, j, t):
                if t < NF:
                    if t == 0:
                        pe.wait_ge(f["x_split"], nth(1, j, 1))
                        if isinstance(j, int) and j == 0 and f is f1:
                            pe.wait_ge(w_free, NP2)
                    pe.wait_ge(f["h_ready"], nth(NF, j, t - 1))
                    bank = f["G"][t % 2]
                    for n, w in enumerate((w_gate, w_up)):
                        for k in range(NK):
                            mm = products(pe, bank[:, n * SEQ:(n + 1) * SEQ], [p[:, k, t * P:(t + 1) * P] for p in w],
                                          [p[:, k, :] for p in f["xT"]], k == 0, k == NK - 1)
                    mm.then_inc(f["gate_up"], 1)
                if t >= 2:
                    d = t - 2
                    pe.wait_ge(f["h_split"], nth(NF, j, d + 1))
                    for b in range(NB):
                        mm = products(pe, f["acc"][:, b * HID:(b + 1) * HID], [p[:, d % 2, b * P:(b + 1) * P] for p in f["hs"]],
                                      [p[:, d, :] for p in w_down], d == 0 and b == 0, d == NF - 1)
                    mm.then_inc(f["down"], 1)

            def ffn_end(f, j):
                pass

            def rwkv(j, n):
                def bank(use):
                    s, per, k = READ[use - 2]
                    pe.wait_ge(s, nth(per, j, k if use >= 2 else k - per))
                    return R[use % 2]

                if n == 2:
                    pe.wait_ge(rn["normed"], nth(3, j, 2))
                    turn(yh, bank(0)).then_inc(turned, 1)
                if n in (5, 6, 7):
                    m = n - 5
                    pe.wait_ge(mix_split, nth(5, j, m + 1))
                    o = bank(1 + m)
                    for c in range(NK):
                        for k in range(NK):
                            mm = products(pe, o[:, c * SEQ:(c + 1) * SEQ], [p[:, k, c * P:(c + 1) * P] for p in w_proj[m]],
                                          [p[:, k, :] for p in mixs[m]], k == 0, k == NK - 1)
                    mm.then_inc(proj, 1)
                if n == 10:
                    pe.wait_ge(o_split, nth(1, j, 1))
                    o = bank(4)
                    for b in range(NB):
                        for k in range(NK):
                            mm = products(pe, o[:, b * HID:(b + 1) * HID], [p[:, k, b * P:(b + 1) * P] for p in mixs[2]],
                                          [p[:, k, :] for p in w_ob], k == 0, k == NK - 1)
                    mm.then_inc(oproj, 1)
                if n == 12:
                    pe.wait_ge(rn["normed"], nth(3, j, 3))
                    turn(yh, bank(5)).then_inc(turned, 1)
                if n in (14, 15, 16, 17):
                    q = n - 14
                    if q == 0:
                        pe.wait_ge(mix_split, nth(5, j, 4))
                    o = bank(6 + q)
                    for e in range(2):
                        for k in range(NK):
                            mm = products(pe, o[:, e * SEQ:(e + 1) * SEQ],
                                          [p[:, k, (2 * q + e) * P:(2 * q + e + 1) * P] for p in w_key],
                                          [p[:, k, :] for p in mixs[0]], k == 0, k == NK - 1)
                    mm.then_inc(key, 1)
                if n == 18:
                    pe.wait_ge(mix_split, nth(5, j, 5))
                    o = bank(10)
                    for b in range(NB):
                        for k in range(NK):
                            mm = products(pe, o[:, b * HID:(b + 1) * HID], [p[:, k, b * P:(b + 1) * P] for p in mixs[1]],
                                          [p[:, k, :] for p in w_cr], k == 0, k == NK - 1)
                    mm.then_inc(cr, 1)
                if n == 19:
                    o = bank(11)
                    for q in range(4):
                        pe.wait_ge(s_split, nth(4, j, q + 1))
                        for c in (2 * q, 2 * q + 1):
                            for b in range(NB):
                                mm = products(pe, o[:, b * HID:(b + 1) * HID], [p[:, c, b * P:(b + 1) * P] for p in ss],
                                              [p[:, c, :] for p in w_val], c == 0 and b == 0, c == NF - 1)
                    mm.then_inc(val, 1)

            run(pe, ffn_prep, ffn_block, ffn_end, rwkv)

        @block.scalar
        def _(act):
            for s in (h_ready, mix_hi, first, exped, rtanh, o_hi, ktanh, s_hi, ctanh,
                      *(f[n] for f in (f1, f2) for n in ("x_hi_ready", "tanh_ready", "h_hi_ready"))):
                act.sem_inc(s, 1)
            for n in range(NP2):
                act.wait_ge(w_loaded[n % ST], 16 * (n // ST + 1))
                for a, b, scale in ranges(n):
                    i_ = act.activation(wt[0][:, n, a:b], stage[n % ST][:, a:b], ACT.Copy, scale=scale)
                i_.then_inc(w_hi, 1)
            act.wait_ge(cols_loaded, 16)

            def ffn_prep(f, j, part):
                if part == 0:
                    return
                act.wait_ge(f["x_turned"], nth(1, j, 1))
                act.wait_ge(f["gate_up"], nth(NF, j, 0))
                act.copy(f["xT"][0][:, :, :].rearrange("p k n -> p (k n)"), f["acc"][:, :]).then_inc(f["x_hi_ready"], 1)

            def ffn_block(f, j, t):
                if t < NF:
                    act.wait_ge(f["gate_up"], nth(NF, j, t + 1))
                    act.wait_ge(f["h_split"], nth(NF, j, t - 1))
                    act.activation(f["h"][:, t % 2, :], f["G"][t % 2][:, 0:SEQ], ACT.Tanh, scale=0.5).then_inc(f["tanh_ready"], 1)
                if 1 <= t <= NF:
                    d = t - 1
                    act.wait_ge(f["h_ready"], nth(NF, j, d + 1))
                    act.wait_ge(f["down"], nth(NF, j, d - 1))
                    act.copy(f["hs"][0][:, d % 2, :], f["h"][:, d % 2, :]).then_inc(f["h_hi_ready"], 1)

            def ffn_end(f, j):
                pass

            def rwkv(j, n):
                def channels(bank, c, gain, shift):
                    act.wait_ge(turned, nth(2, j, c + 1))
                    act.wait_ge(mixed, nth(5, j, -1 + 1 if c == 0 else 3))
                    for k in range(NK):
                        a = act.activation(hT[:, k, 1:SEQ + 1], bank[:, k * SEQ:(k + 1) * SEQ], ACT.Identity,
                                           scale=cols[:, gain, k:k + 1], bias=cols[:, shift, k:k + 1])
                    a.then_inc(h_ready, 1)

                def hi_mix(m):
                    act.wait_ge(mixed, nth(5, j, m + 1))
                    if m == 0:
                        act.wait_ge(key, nth(4, j, 0))
                    if m == 1:
                        act.wait_ge(cr, nth(1, j, 0))
                    if m == 2:
                        act.wait_ge(oproj, nth(1, j, 0))
                    if m in (3, 4):
                        act.wait_ge(proj, nth(3, j, m - 2))
                    dst = mixs[m if m < 3 else m - 3][0]
                    act.copy(dst[:, :, :], mixf[:, m % 2 if m < 3 else m - 3, :, :]).then_inc(mix_hi, 1)

                if n == 2:
                    channels(R[0], 0, LG1, LB1)
                if n in (3, 4, 5):
                    hi_mix(n - 3)
                if n == 6:
                    act.wait_ge(proj, nth(3, j, 1))
                    act.wait_ge(av, nth(1, j, 0))
                    for c in range(NK):
                        a = act.activation(e2[:, c, :], R[1][:, c * SEQ:(c + 1) * SEQ], ACT.Identity, scale=1.0,
                                           bias=cols[:, FIRST, c:c + 1])
                    a.then_inc(first, 1)
                if n == 7:
                    act.wait_ge(floored, nth(1, j, 1))
                    act.activation(e2[:, :, :], e2[:, :, :], ACT.Exp).then_inc(exped, 1)
                if n == 8:
                    act.wait_ge(proj, nth(3, j, 3))
                    act.wait_ge(u_ready, nth(1, j, 0))
                    act.activation(th[:, :, :].rearrange("p a b -> p (a b)"), R[1][:, :], ACT.Tanh,
                                   scale=0.5).then_inc(rtanh, 1)
                if n == 9:
                    act.wait_ge(o_ready, nth(1, j, 1))
                    act.wait_ge(proj, nth(3, j, 3))
                    act.copy(mixs[2][0][:, :, :], mixf[:, 1, :, :]).then_inc(o_hi, 1)
                if n == 12:
                    channels(R[1], 1, LG2, LB2)
                if n == 13:
                    hi_mix(3)
                    hi_mix(4)
                if 14 <= n <= 17:
                    q = n - 14
                    act.wait_ge(key, nth(4, j, q + 1))
                    if q:
                        act.wait_ge(s_ready, nth(4, j, q))
                    else:
                        act.wait_ge(o_ready, nth(1, j, 1))
                    act.activation(th[:, :, :].rearrange("p a b -> p (a b)"), R[q % 2][:, :], ACT.Tanh,
                                   scale=0.5).then_inc(ktanh, 1)
                if 15 <= n <= 18:
                    q = n - 15
                    act.wait_ge(s_ready, nth(4, j, q + 1))
                    if q == 0:
                        act.wait_ge(val, nth(1, j, 0))
                    act.copy(ss[0][:, 2 * q:2 * q + 2, :], mixf[:, q % 2, :, :]).then_inc(s_hi, 1)
                if n == 18:
                    act.wait_ge(cr, nth(1, j, 1))
                    act.activation(th[:, :, :].rearrange("p a b -> p (a b)"), R[0][:, :], ACT.Tanh,
                                   scale=0.5).then_inc(ctanh, 1)

            run(act, ffn_prep, ffn_block, ffn_end, rwkv)

        @block.gpsimd
        def _(pool):
            for s in (rn, f1["norm"], f2["norm"]):
                pool.sem_inc(s["rstd_ready"], 1)
            pool.memset(half[:, :], -0.5).then_inc(made, 1)
            pool.wait_ge(made, 1)

            def root(s, per, j, n):
                pool.wait_ge(s["var_ready"], nth(per, j, n + 1))
                pool.tensor_tensor(s["rstd"][:, :], s["ve"][:, :], half[:, :], ALU.pow).then_inc(s["rstd_ready"], 1)

            def ffn_prep(f, j, part):
                if part == 0:
                    root(f["norm"], 1, j, 0)

            def rwkv(j, n):
                if n in (0, 1, 11):
                    root(rn, 3, j, {0: 0, 1: 1, 11: 2}[n])

            run(pool, ffn_prep, lambda f, j, t: None, lambda f, j: None, rwkv)

        @block.vector
        def _(dve):
            for s in (diffed, mixed, mix_split, floored, recip, av, wkv, o_ready, o_split, y_added, xy_added, s_ready,
                      s_split, u_ready, x_added,
                      *(f[n] for f in (f1, f2) for n in ("x_split", "added", "gated", "h_ready", "h_split")),
                      *(f[n] for f in (rn, f1["norm"], f2["norm"])
                        for n in ("stats_made", "aggregated", "var_ready", "normed"))):
                dve.sem_inc(s, 1)
            for n in range(NP2):
                dve.wait_ge(w_hi, n + 1)
                for a, b, scale in ranges(n):
                    i_ = dve.scalar_tensor_tensor(wt[1][:, n, a:b], stage[n % ST][:, a:b], scale,
                                                  wt[0][:, n, a:b].bitcast(F32), ALU.mult, ALU.subtract)
                i_.then_inc(w_free, 1)
            for k in range(NK):
                a = dve.memset(hT[:, k, 0:1], 0.0)
            a.then_inc(made_h, 1)
            dve.wait_ge(made_h, 1)
            dve.wait_ge(cols_loaded, 16)

            def measure(s, per, j, n, src):
                for b in range(NB):
                    a = dve.bn_stats(s["stats"][:, b, :], src(b))
                a.then_inc(s["stats_made"], 1)
                dve.wait_ge(s["stats_made"], nth(per, j, n + 1))
                dve.memset(s["spare"][:, :], 0.0)
                for b in range(NB):
                    a = dve.bn_aggr(s["mv"][:, b, :], s["stats"][:, b, :])
                a.then_inc(s["aggregated"], 1)
                dve.wait_ge(s["aggregated"], nth(per, j, n + 1))
                dve.tensor_scalar(s["ve"][:, :], s["mv"][:, :, 1], EPS, None, ALU.add).then_inc(s["var_ready"], 1)

            def apply(s, per, j, n, src, dst):
                dve.wait_ge(s["rstd_ready"], nth(per, j, n + 1))
                for b in range(NB):
                    a = dve.tensor_scalar(dst(b), src(b), s["mv"][:, b, 0:1], s["rstd"][:, b:b + 1], ALU.subtract,
                                          ALU.mult)
                a.then_inc(s["normed"], 1)

            def ffn_prep(f, j, part):
                if part == 0:
                    if f is f2:
                        dve.wait_ge(x_added, nth(1, j, 1))
                    measure(f["norm"], 1, j, 0, lambda b: rows(j, b))
                else:
                    dve.wait_ge(f["x_turned"], nth(1, j, 0))
                    apply(f["norm"], 1, j, 0, lambda b: rows(j, b), lambda b: f["xhat"][:, b, :])
                    dve.wait_ge(f["x_hi_ready"], nth(1, j, 1))
                    dve.tensor_tensor(f["xT"][1][:, :, :].rearrange("p k n -> p (k n)"), f["acc"][:, :],
                                      f["xT"][0][:, :, :].rearrange("p k n -> p (k n)").bitcast(F32),
                                      ALU.subtract).then_inc(f["x_split"], 1)

            def ffn_block(f, j, t):
                if t < NF:
                    dve.wait_ge(f["tanh_ready"], nth(NF, j, t + 1))
                    h = f["h"][:, t % 2, :]
                    dve.scalar_tensor_tensor(h, h, 1.0, f["G"][t % 2][:, 0:SEQ], ALU.add, ALU.mult).then_inc(f["gated"], 1)
                    dve.wait_ge(f["gated"], nth(NF, j, t + 1))
                    dve.tensor_tensor(h, h, f["G"][t % 2][:, SEQ:2 * SEQ], ALU.mult).then_inc(f["h_ready"], 1)
                if 1 <= t <= NF:
                    d = t - 1
                    dve.wait_ge(f["h_hi_ready"], nth(NF, j, d + 1))
                    dve.tensor_tensor(f["hs"][1][:, d % 2, :], f["h"][:, d % 2, :], f["hs"][0][:, d % 2, :].bitcast(F32),
                                      ALU.subtract).then_inc(f["h_split"], 1)

            def ffn_end(f, j):
                dve.wait_ge(f["down"], nth(NF, j, NF))
                dve.tensor_tensor(rows(j, 0, NB), f["acc"][:, :], rows(j, 0, NB), ALU.add).then_inc(f["added"], 1)

            def rwkv(j, n):
                def mix(m, row):
                    sem_, per, k = [(x_added, 1, 0), (s_split, 4, 0), (mix_split, 5, 1), (mix_split, 5, 3),
                                    (o_split, 1, 1)][m]
                    dve.wait_ge(sem_, nth(per, j, k))
                    for k in range(NK):
                        a = dve.scalar_tensor_tensor(mixf[:, m % 2 if m < 3 else m - 3, k, :], diff[:, k, :],
                                                     cols[:, row, k:k + 1], hT[:, k, 0:SEQ], ALU.mult, ALU.add)
                    a.then_inc(mixed, 1)

                def lo_mix(m):
                    dve.wait_ge(mix_hi, nth(5, j, m + 1))
                    s = mixs[m if m < 3 else m - 3]
                    dve.tensor_tensor(s[1][:, :, :], mixf[:, m % 2 if m < 3 else m - 3, :, :], s[0][:, :, :].bitcast(F32),
                                      ALU.subtract).then_inc(mix_split, 1)

                def difference(c):
                    dve.wait_ge(h_ready, nth(2, j, c + 1))
                    dve.tensor_tensor(diff, hT[:, :, 1:SEQ + 1], hT[:, :, 0:SEQ], ALU.subtract).then_inc(diffed, 1)
                    dve.wait_ge(diffed, nth(2, j, c + 1))

                if n == 0:
                    dve.wait_ge(f1["added"], nth(1, j, 1))
                    measure(rn, 3, j, 0, lambda b: rows(j, b))
                if n == 1:
                    apply(rn, 3, j, 0, lambda b: rows(j, b), lambda b: y[:, b, :])
                    dve.wait_ge(rn["normed"], nth(3, j, 1))
                    measure(rn, 3, j, 1, lambda b: y[:, b, :])
                if n == 2:
                    dve.wait_ge(turned, nth(2, j, 0))
                    dve.wait_ge(mixed, nth(5, j, 0))
                    dve.wait_ge(rn["stats_made"], nth(3, j, 2))
                    apply(rn, 3, j, 1, lambda b: y[:, b, :], lambda b: yh[:, b, :])
                if n == 3:
                    difference(0)
                    mix(0, MK)
                    mix(1, MV)
                    lo_mix(0)
                if n == 4:
                    mix(2, MR)
                    lo_mix(1)
                if n == 5:
                    lo_mix(2)
                if n == 6:
                    dve.wait_ge(first, nth(1, j, 1))
                    dve.tensor_scalar(e2[:, :, :], e2[:, :, :], PP0, 0.0, ALU.subtract, ALU.min).then_inc(floored, 1)
                if n == 7:
                    dve.wait_ge(exped, nth(1, j, 1))
                    dve.reciprocal(ri[:, :, :], e2[:, :, :]).then_inc(recip, 1)
                    dve.wait_ge(proj, nth(3, j, 2))
                    dve.wait_ge(recip, nth(1, j, 1))
                    dve.tensor_tensor(e2[:, :, :].rearrange("p a b -> p (a b)"), R[0][:, :],
                                      e2[:, :, :].rearrange("p a b -> p (a b)"), ALU.mult).then_inc(av, 1)
                    dve.wait_ge(av, nth(1, j, 1))
                    dve.tensor_tensor(ri[:, :, :], e2[:, :, :], ri[:, :, :], ALU.mult).then_inc(wkv, 1)
                if n == 8:
                    dve.wait_ge(rtanh, nth(1, j, 1))
                    dve.wait_ge(wkv, nth(1, j, 1))
                    dve.wait_ge(mix_split, nth(5, j, 2))
                    dve.scalar_tensor_tensor(mixf[:, 1, :, :], th[:, :, :], 1.0, ri[:, :, :], ALU.add,
                                             ALU.mult).then_inc(o_ready, 1)
                if n == 9:
                    dve.wait_ge(o_hi, nth(1, j, 1))
                    dve.tensor_tensor(mixs[2][1][:, :, :], mixf[:, 1, :, :], mixs[2][0][:, :, :].bitcast(F32),
                                      ALU.subtract).then_inc(o_split, 1)
                if n == 10:
                    dve.wait_ge(oproj, nth(1, j, 1))
                    yf = y[:, :, :].rearrange("p b c -> p (b c)")
                    dve.tensor_tensor(yf, R[0][:, :], yf, ALU.add).then_inc(y_added, 1)
                    dve.wait_ge(y_added, nth(1, j, 1))
                    measure(rn, 3, j, 2, lambda b: y[:, b, :])
                    dve.tensor_tensor(rows(j, 0, NB), yf, rows(j, 0, NB), ALU.add).then_inc(xy_added, 1)
                if n == 12:
                    dve.wait_ge(mixed, nth(5, j, 3))
                    apply(rn, 3, j, 2, lambda b: y[:, b, :], lambda b: yh[:, b, :])
                if n == 13:
                    difference(1)
                    mix(3, CK)
                    mix(4, CR)
                    lo_mix(3)
                    lo_mix(4)
                if 14 <= n <= 17:
                    q = n - 14
                    dve.wait_ge(ktanh, nth(4, j, q + 1))
                    if q < 2:
                        dve.wait_ge(mix_split, nth(5, j, 4 + q))
                    else:
                        dve.wait_ge(s_split, nth(4, j, q - 1))
                    dve.scalar_tensor_tensor(mixf[:, q % 2, :, :], th[:, :, :], 1.0,
                                             R[q % 2][:, :].rearrange("p (a b) -> p a b", a=2), ALU.add,
                                             ALU.mult).then_inc(s_ready, 1)
                if 15 <= n <= 18:
                    q = n - 15
                    dve.wait_ge(s_hi, nth(4, j, q + 1))
                    dve.tensor_tensor(ss[1][:, 2 * q:2 * q + 2, :], mixf[:, q % 2, :, :],
                                      ss[0][:, 2 * q:2 * q + 2, :].bitcast(F32), ALU.subtract).then_inc(s_split, 1)
                if n == 19:
                    dve.wait_ge(ctanh, nth(1, j, 1))
                    dve.wait_ge(val, nth(1, j, 1))
                    dve.wait_ge(s_split, nth(4, j, 3))
                    dve.scalar_tensor_tensor(mixf[:, 0, :, :].rearrange("p a b -> p (a b)"),
                                             th[:, :, :].rearrange("p a b -> p (a b)"), 1.0, R[1][:, :], ALU.add,
                                             ALU.mult).then_inc(u_ready, 1)
                    dve.wait_ge(u_ready, nth(1, j, 1))
                    dve.tensor_tensor(rows(j, 0, NB), mixf[:, 0, :, :].rearrange("p a b -> p (a b)"), rows(j, 0, NB),
                                      ALU.add).then_inc(x_added, 1)

            run(dve, ffn_prep, ffn_block, ffn_end, rwkv)


_INS = ["x_in", "w_group", "w_out", "qg", "qb", "kg", "kb", "cos_t", "sin_t", "ident_in", "identb_in", "mask_in",
        "w_tail", "cols_in"]


def kernel(**inp):
    import ml_dtypes
    import numpy as np
    import concourse.bacc as bacc
    from concourse import mybir as mb
    from concourse.bass_utils import run_bass_kernel_spmd

    a = {k: np.asarray(v) for k, v in inp.items()}
    wqkv = a["L0_attn_a_w_qkv"]
    q, k, v = wqkv[:HEADS * D], wqkv[HEADS * D:(HEADS + KV) * D], wqkv[(HEADS + KV) * D:]
    grouped = np.concatenate([q.reshape(NG, QC, HID), k.reshape(NG, D, HID), v.reshape(NG, D, HID)], 1)
    w_group = grouped.reshape(NG, GW, NK, P).transpose(2, 0, 3, 1)
    w_out = a["L0_attn_a_w_o"].reshape(HID, HEADS, D).transpose(2, 1, 0)
    freq = (1.0 / np.float32(1000000.0) ** (np.arange(0, D, 2, dtype=np.float32) / np.float32(D))).astype(np.float32)
    ang = np.outer(np.arange(SEQ, dtype=np.float32), freq).astype(np.float32)
    cos, sin = np.cos(ang), np.sin(ang)
    tri = np.where(np.arange(P)[None, :] > np.arange(P)[:, None], np.float32(MASKED), np.float32(0.0))
    def turned(name, chunks):
        w = a[name]
        return w.T.reshape(chunks, P, w.shape[0]).transpose(1, 0, 2).reshape(P, -1)

    b = "L0_attn_b_"
    w_tail = np.concatenate([turned("L0_ffn_w_gate", NK), turned("L0_ffn_w_up", NK), turned("L0_ffn_w_down", NF),
                             turned(b + "Wkey", NK), turned(b + "Wval", NF), turned(b + "Wk", NK), turned(b + "Wv", NK),
                             turned(b + "Wr", NK), turned(b + "Wo", NK), turned(b + "Wcr", NK),
                             np.zeros((P, BANK), np.float32)], 1).reshape(P, NP2, PW)
    cols_in = np.stack([a[b + n].reshape(NK, P).T for n in
                        ("ln1_g", "ln1_b", "ln2_g", "ln2_b", "tm_first", "tm_mk", "tm_mv", "tm_mr", "cm_mk", "cm_mr")], 1)
    arrays = {
        "w_tail": w_tail, "cols_in": cols_in,
        "x_in": a["L0_attn_a_x"], "w_group": w_group, "w_out": w_out,
        "qg": a["L0_attn_a_qn_g"], "qb": a["L0_attn_a_qn_b"], "kg": a["L0_attn_a_kn_g"], "kb": a["L0_attn_a_kn_b"],
        "cos_t": np.concatenate([cos, cos], 1), "sin_t": np.concatenate([sin, -sin], 1),
        "ident_in": np.eye(P, dtype=np.float32), "identb_in": np.eye(P, dtype=ml_dtypes.bfloat16),
        "mask_in": tri.astype(ml_dtypes.bfloat16),
    }
    nc = bacc.Bacc("TRN2", target_bir_lowering=False, num_devices=1)
    arrays = {n: np.ascontiguousarray(arrays[n]) for n in _INS}
    aps = [nc.dram_tensor(n, arrays[n].shape, mb.dt.from_np(arrays[n].dtype), kind="ExternalInput").ap() for n in _INS]
    out = nc.dram_tensor("out", (NSEQ, SEQ, HID), mb.dt.float32, kind="ExternalOutput").ap()
    kernel_program(nc, *aps, out)
    r = run_bass_kernel_spmd(nc, [arrays], core_ids=[0])
    return r.results[0]["out"]
```

```python
from contextlib import ExitStack

import concourse.bass as bass
from concourse import mybir

F32 = mybir.dt.float32
F32R = mybir.dt.float32r
BF16 = mybir.dt.bfloat16
ALU = mybir.AluOpType
ACT = mybir.ActivationFunctionType
AX = mybir.AxisListType

P = 128
NSEQ, SEQ, HID = 16, 256, 256
NB = SEQ // P
NK = HID // P
HEADS, KV, D = 16, 4, 128
REP = HEADS // KV
NG = KV
GW = (REP + 2) * D
QC = REP * D
FF = 1024
NF = FF // P
EPS = 1e-5
MASKED = -1e30
BANK = 512


def nth(per, i, k):
    value = i * per + k + 1
    return max(value, 1) if isinstance(value, int) else value


def products(pe, out, lhs, rhs, first, last):
    passes = ((0, 0), (0, 1), (1, 0))
    for n, (a, b) in enumerate(passes):
        mm = pe.matmul(out, lhs[a], rhs[b], start=first and n == 0, stop=last and n == 2, skip_group_check=True)
    return mm


def kernel_program(nc, x_in, w_group, w_out, qg, qb, kg, kb, cos_t, sin_t, ident_in, identb_in, mask_in,
                   w_tail, cols_in, out):
    ctx = ExitStack()
    with ctx:
        def sb(name, shape, dt=F32, c=ctx):
            return c.enter_context(nc.sbuf_tensor(name, shape, dt))

        def sem(name):
            return ctx.enter_context(nc.semaphore(name))

        x = sb("x", [P, NSEQ * NB, HID])
        ident = sb("ident", [P, P])
        banks = [ctx.enter_context(nc.psum_tensor(f"bank{n}", [P, BANK], F32)) for n in range(8)]
        x_loaded = [sem("x_first_loaded"), sem("x_rest_loaded")]
        const_loaded = sem("const_loaded")
        with ExitStack() as mem:
            attention(nc, lambda n, s, d=F32: sb(n, s, d, mem), sem, banks, x, ident, x_loaded, const_loaded,
                      x_in, w_group, w_out, qg, qb, kg, kb, cos_t, sin_t, ident_in, identb_in, mask_in)
        with ExitStack() as mem:
            tail(nc, lambda n, s, d=F32: sb(n, s, d, mem), sem, banks, x, ident, w_tail, cols_in)
        store(nc, sem, x, out)


def store(nc, sem, x, out):
    stored = sem("stored")
    with nc.Block() as block:
        @block.sync
        def _(sp):
            sp.dma_start(out.rearrange("s (b p) c -> p (s b) c", p=P), x[:, :, :]).then_inc(stored, 16)
            sp.wait_ge(stored, 16)


def attention(nc, sb, sem, banks, x, ident, x_loaded, const_loaded,
              x_in, w_group, w_out, qg, qb, kg, kb, cos_t, sin_t, ident_in, identb_in, mask_in):
    wg = [sb(f"wg_{p}", [P, NK, NG, GW], F32R) for p in ("hi", "lo")]
    wo = [sb(f"wo_{p}", [P, HEADS, HID], F32R) for p in ("hi", "lo")]
    identb = sb("identb", [P, P], BF16)
    mask = sb("mask", [P, P], BF16)
    cos = sb("cos", [P, NB, D])
    sin = sb("sin", [P, NB, D])
    gain = sb("gain", [P, 2, D])
    bias = sb("bias", [P, 2, D])
    tabA = sb("tabA", [P, 2, NB, D])
    tabB = sb("tabB", [P, 2, NB, D])
    tabC = sb("tabC", [P, 2, NB, D])
    xhat = sb("xhat", [P, NB, HID])
    ln_stats = sb("ln_stats", [P, NB, 6])
    ln_mv = sb("ln_mv", [P, NB, 2])
    ln_ve = sb("ln_ve", [P, NB])
    ln_rstd = sb("ln_rstd", [P, NB])
    spare = sb("spare", [P, 1])
    deps = sb("deps", [P, REP])
    half = sb("half", [P, 8])
    xT = [sb(f"xT_{p}", [P, NK, SEQ], F32R) for p in ("hi", "lo")]
    sq = sb("sq", [P, 3, QC])
    ssum = sb("ssum", [P, 3, REP])
    ve = sb("ve", [P, 3, REP])
    rstd = sb("rstd", [P, 3, REP])
    qn = sb("qn", [P, 3, QC])
    m1 = sb("m1", [P, 3, QC])
    m2 = sb("m2", [P, 3, QC])
    v = [sb(f"v_{p}", [P, NG, NB, D], F32R) for p in ("hi", "lo")]
    qT = [sb(f"qT_{p}", [P, 3, QC], F32R) for p in ("hi", "lo")]
    probs = sb("probs", [P, 3, BANK])
    negmax = sb("negmax", [P, 8])
    psum_ = sb("rowsum", [P, 8])
    rinv = sb("rinv", [P, 8])
    pT = [sb(f"pT_{p}", [P, 3, REP, P], F32R) for p in ("hi", "lo")]
    oT = [sb(f"oT_{p}", [P, NB, REP, P], F32R) for p in ("hi", "lo")]

    A = banks[0:2]
    T = banks[2:5]
    S = banks[5:7]
    W = banks[7]
    UA, US = 3, 3
    UT = 8 * NG + 1

    w_loaded = [sem(f"w_loaded{n}") for n in range(6)]
    w_hi, w_free = sem("w_hi"), sem("w_free")
    tab = sem("tab")
    const_made = sem("const_made")
    ln_s, ln_a = sem("ln_stats_made"), sem("ln_aggregated")
    ln_v, ln_r, ln_x = sem("ln_var_ready"), sem("ln_rstd_ready"), sem("xhat_ready")
    qkv_ready, sq_ready, var_ready = sem("qkv_ready"), sem("sq_ready"), sem("var_ready")
    rstd_ready, qn_ready, m1_ready, m2_ready = sem("rstd_ready"), sem("qn_ready"), sem("m1_ready"), sem("m2_ready")
    rot_ready = sem("rotated")
    v_hi, v_ready = sem("v_hi_ready"), sem("v_ready")
    t_ready, t_hi, t_split = sem("t_ready"), sem("t_hi"), sem("t_split")
    s_ready, s_max, s_exp = sem("s_ready"), sem("s_max_ready"), sem("s_exp_ready")
    r_ready, p_ready = sem("rinv_ready"), sem("probs_ready")
    wo_ready, wo_added = sem("wo_ready"), sem("wo_added")

    def skip(eng, s, i, g, use, n):
        if i == NSEQ and g > 1:
            return
        eng.wait_ge(s, nth(UT, i, 1 + use))
        eng.sem_inc(s, n)

    def real(i, g, lag):
        t = None if not isinstance(i, int) else NG * i + g - lag
        return (t is None or 0 <= t < NG * NSEQ), (g - lag) % NG

    def step(i, g, lag):
        return (i, g - lag)

    def more(i):
        return not isinstance(i, int) or i < NSEQ - 1

    def use_qk(g): return 8 * g
    def use_p(g): return 8 * g + 3
    def use_x(): return 8 * (NG - 1) + 6
    def use_o(g): return 8 * g + 6 + (g == NG - 1)

    SEQ0 = NSEQ

    def run(eng, body, before):
        before()
        for g in range(NG):
            body(0, g)
        with eng.Fori(1, NSEQ - 1) as i:
            for g in range(NG):
                body(i, g)
        for g in range(NG):
            body(NSEQ - 1, g)
        for g in range(3):
            body(NSEQ, g)

    STG = 6
    stage = [t[:, :, :].rearrange("p a b -> p (a b)")[:, n * GW:(n + 1) * GW] for t in (sq, qn, probs) for n in range(2)]
    pieces = [("g", k, g) for k in range(NK) for g in range(NG)] + [("o", h, min(3, HEADS - h)) for h in range(0, HEADS, 3)]

    def piece_ap(n, part):
        kind, a, b = pieces[n]
        return wg[part][:, a, b, :] if kind == "g" else wo[part][:, a:a + b, :].rearrange("p h n -> p (h n)")

    def piece_stage(n):
        kind, a, b = pieces[n]
        return stage[n % STG][:, 0:GW if kind == "g" else b * HID]

    csum = sb("csum", [P, REP + 1])
    cent = sem("centred")

    with nc.Block() as block:
        @block.sync
        def _(sp):
            xv = x_in.rearrange("s (b p) c -> p (s b) c", p=P)
            sp.dma_start(x[:, 0:NB, :], xv[:, 0:NB, :]).then_inc(x_loaded[0], 16)
            for n in range(len(pieces)):
                kind, a, b = pieces[n]
                if n == 2:
                    for dst, src in ((ident[:, :], ident_in), (identb[:, :], identb_in),
                                     (mask[:, :], mask_in),
                                     (cos[:, :, :], cos_t.rearrange("(b p) d -> p b d", p=P)),
                                     (sin[:, :, :], sin_t.rearrange("(b p) d -> p b d", p=P)),
                                     (gain[:, 0, :], qg.partition_broadcast(P)), (gain[:, 1, :], kg.partition_broadcast(P)),
                                     (bias[:, 0, :], qb.partition_broadcast(P)), (bias[:, 1, :], kb.partition_broadcast(P))):
                        sp.dma_start(dst, src).then_inc(const_loaded, 16)
                if n >= STG:
                    sp.wait_ge(w_free, n - STG + 1)
                src = w_group[a, b] if kind == "g" else w_out[:, a:a + b, :].rearrange("p h n -> p (h n)")
                sp.dma_start(piece_stage(n), src).then_inc(w_loaded[n % STG], 16)
            sp.dma_start(x[:, NB:, :], xv[:, NB:, :]).then_inc(x_loaded[1], 16)

        @block.tensor
        def _(pe):
            def begin():
                for s in (qkv_ready, t_ready, s_ready, wo_ready):
                    pe.sem_inc(s, 1)
                pe.wait_ge(const_loaded, 9 * 16)
                turn_x(0)

            def turn_x(i):
                pe.wait_ge(ln_x, nth(1, i, 1))
                for k in range(NK):
                    for b in range(NB):
                        mm = pe.transpose(T[xbank][:, (k * NB + b) * P:(k * NB + b + 1) * P],
                                          xhat[:, b, k * P:(k + 1) * P], ident[:, :])
                mm.then_inc(t_ready, 1)

            xbank = use_x() % 3

            def body(i, g):
                def project(u):
                    bank = A[(UA * g + u) % 2]
                    pe.wait_ge(qn_ready, nth(UA * NG, i, UA * g + u - 1))
                    if g == 0 and u == 0:
                        pe.wait_ge(t_split, nth(UT, i, 1))
                    if not isinstance(i, int) or i == 0:
                        if u == 0 and isinstance(i, int):
                            pe.wait_ge(w_free, 2 * NG)
                    for b in ((u,) if u < 2 else (0, 1)):
                        for k in range(NK):
                            cols = slice(0, QC) if u < 2 else slice(QC, GW)
                            o = bank[:, :] if u < 2 else bank[:, b * 2 * D:(b + 1) * 2 * D]
                            mm = products(pe, o, [w[:, k, b * P:(b + 1) * P] for w in xT],
                                          [w[:, k, g, cols] for w in wg], k == 0, k == NK - 1)
                    mm.then_inc(qkv_ready, 1)

                def turn_qk():
                    ok, _ = real(i, g, 1)
                    if not ok:
                        return skip(pe, t_ready, i, g, use_qk(g), 3)
                    for u in range(3):
                        use = use_qk(g) + u
                        pe.wait_ge(rot_ready, nth(UA * NG, i, UA * (g - 1) + u + 1))
                        pe.wait_ge(t_split, nth(UT, i, 1 + use - 2))
                        for h in range(REP if u < 2 else NB):
                            o = T[use % 3][:, h * P:(h + 1) * P]
                            c = tabC[:, 0, u, :] if u < 2 else tabC[:, 1, h, :]
                            for n, src in enumerate((m1[:, u, h * D:(h + 1) * D], c)):
                                mm = pe.matmul(o, src, ident[:, :], is_transpose=True, start=n == 0, stop=n == 1,
                                               skip_group_check=True)
                        mm.then_inc(t_ready, 1)

                def turn_probs():
                    ok, _ = real(i, g, 2)
                    if not ok:
                        return skip(pe, t_ready, i, g, use_p(g), 3)
                    pe.wait_ge(p_ready, nth(NG, i, g - 2 + 1))
                    for u in range(3):
                        use = use_p(g) + u
                        pe.wait_ge(t_split, nth(UT, i, 1 + use - 2))
                        for h in range(REP):
                            src = (probs[:, 0, h * P:(h + 1) * P] if u == 0 else
                                   probs[:, 1 + h // 2, (h % 2) * SEQ + (u - 1) * P:(h % 2) * SEQ + u * P])
                            mm = pe.transpose(T[use % 3][:, h * P:(h + 1) * P], src, ident[:, :])
                        mm.then_inc(t_ready, 1)

                def scores(u):
                    if not real(i, g, 1)[0]:
                        return
                    if u == 0:
                        pe.wait_ge(t_split, nth(UT, i, 1 + use_qk(g) + 3))
                    bank = S[(US * (g - 1) + u) % 2]
                    pe.wait_ge(s_exp, nth(US * NG, i, US * (g - 1) + u - 1))
                    keys, heads = (P, range(REP)) if u == 0 else (SEQ, range(2 * u - 2, 2 * u))
                    for n, h in enumerate(heads):
                        o = bank[:, n * keys:(n + 1) * keys]
                        products(pe, o, [w[:, min(u, 1), h * P:(h + 1) * P] for w in qT],
                                 [w[:, 2, 0:keys] for w in qT], True, False)
                        mm = pe.matmul(o[:, keys - P:keys], identb[:, :], mask[:, :], start=False, stop=True,
                                       skip_group_check=True)
                    mm.then_inc(s_ready, 1)

                def sums():
                    ok, gv = real(i, g, 2)
                    if not ok:
                        return skip(pe, t_ready, i, g, use_o(g), 2)
                    pe.wait_ge(t_split, nth(UT, i, 1 + use_p(g) + 3))
                    pe.wait_ge(v_ready, nth(NG, i, g - 2 + 1))
                    for b in range(NB):
                        use = use_o(g) + b
                        pe.wait_ge(t_split, nth(UT, i, 1 + use - 2))
                        for kb_ in range(b + 1):
                            mm = products(pe, T[use % 3][:, :], [w[:, gv, kb_, :] for w in v],
                                          [w[:, b + kb_, :, :].rearrange("p h q -> p (h q)") for w in pT],
                                          kb_ == 0, kb_ == b)
                        mm.then_inc(t_ready, 1)

                def project_out():
                    ok, go = real(i, g, 3)
                    if not ok:
                        return
                    pe.wait_ge(t_split, nth(UT, i, 1 + (use_o(g - 1) + 2 if g else use_o(NG - 1) + 2 - UT)))
                    if go == 0:
                        if isinstance(i, int) and i == 0:
                            pe.wait_ge(w_free, len(pieces))
                        pe.wait_ge(wo_added, nth(1, i, 0 if g == 3 else -1))
                    for b in range(NB):
                        for h in range(REP):
                            mm = products(pe, W[:, b * HID:(b + 1) * HID], [w[:, b, h, :] for w in oT],
                                          [w[:, go * REP + h, :] for w in wo],
                                          go == 0 and b == 0 and h == 0, go == NG - 1 and h == REP - 1)
                    if go == NG - 1:
                        mm.then_inc(wo_ready, 1)

                new = not isinstance(i, int) or i < NSEQ
                if new:
                    project(0)
                    project(1)
                turn_qk()
                project_out()
                turn_probs()
                scores(0)
                scores(1)
                if new:
                    project(2)
                if g == NG - 1:
                    turn_x_next(i)
                scores(2)
                sums()

            def turn_x_next(i):
                pe.wait_ge(t_split, nth(UT, i, 1 + use_x() - 2))
                turn_x(i + 1 if more(i) else i)

            run(pe, body, begin)

        @block.scalar
        def _(act):
            def begin():
                for s in (sq_ready, qn_ready, v_hi, t_hi, s_exp):
                    act.sem_inc(s, 1)
                for n in range(len(pieces)):
                    act.wait_ge(w_loaded[n % STG], 16 * (n // STG + 1))
                    if pieces[n][0] == "g":
                        act.wait_ge(cent, 2 * (n + 1))
                    act.copy(piece_ap(n, 0), piece_stage(n)).then_inc(w_hi, 1)
                    if n == 2 * NG - 1:
                        split_hi(0, 0, xT[0][:, :, :].rearrange("p k n -> p (k n)"), xb)

            xb = use_x() % 3

            def split_hi(i, count, dst, bank, width=BANK):
                act.wait_ge(t_ready, nth(UT, i, count + 1))
                act.copy(dst, T[bank][:, 0:width]).then_inc(t_hi, 1)

            def body(i, g):
                def square(u):
                    act.wait_ge(qkv_ready, nth(UA * NG, i, UA * g + u + 1))
                    act.wait_ge(rstd_ready, nth(UA * NG, i, UA * (g - 1) + u + 1))
                    if isinstance(i, int) and i == 0 and g == 0 and u == 0:
                        act.wait_ge(w_free, len(pieces))
                    bank = A[(UA * g + u) % 2]
                    for h in range(REP if u < 2 else NB):
                        at = h * D if u < 2 else h * 2 * D
                        a = act.activation(sq[:, u, h * D:(h + 1) * D], bank[:, at:at + D], ACT.Square,
                                           accum_out=ssum[:, u, h:h + 1])
                    a.then_inc(sq_ready, 1)
                    if u == 2:
                        kv = bank[:, :].rearrange("p (b s d) -> p b s d", b=NB, s=2)
                        act.wait_ge(t_ready, nth(UT, i, 1 + 8 * g - 8))
                        act.copy(v[0][:, g, :, :], kv[:, :, 1, :]).then_inc(v_hi, 1)

                def normalise(u):
                    if u == 2:
                        act.wait_ge(v_ready, nth(NG, i, g + 1))
                    act.wait_ge(rstd_ready, nth(UA * NG, i, UA * g + u + 1))
                    act.wait_ge(rot_ready, nth(UA * NG, i, UA * (g - 1) + u + 1))
                    bank = A[(UA * g + u) % 2]
                    for h in range(REP if u < 2 else NB):
                        at = h * D if u < 2 else h * 2 * D
                        a = act.activation(qn[:, u, h * D:(h + 1) * D], bank[:, at:at + D], ACT.Copy,
                                           scale=rstd[:, u, h:h + 1])
                    a.then_inc(qn_ready, 1)

                def hi_qk():
                    if not real(i, g, 1)[0]:
                        return skip(act, t_hi, i, g, use_qk(g), 3)
                    act.wait_ge(s_ready, nth(US * NG, i, US * (g - 1)))
                    for u in range(3):
                        w = QC if u < 2 else NB * P
                        split_hi(i, 1 + use_qk(g) + u, qT[0][:, u, 0:w], (use_qk(g) + u) % 3, w)

                def hi_probs():
                    if not real(i, g, 2)[0]:
                        return skip(act, t_hi, i, g, use_p(g), 3)
                    for u in range(3):
                        split_hi(i, 1 + use_p(g) + u, pT[0][:, u, :, :].rearrange("p h q -> p (h q)"), (use_p(g) + u) % 3)

                def exps(u):
                    if not real(i, g, 1)[0]:
                        return
                    if u == 0:
                        act.wait_ge(t_ready, nth(UT, i, 1 + use_p(g) + 3))
                    act.wait_ge(s_max, nth(US * NG, i, US * (g - 1) + u + 1))
                    bank = S[(US * (g - 1) + u) % 2]
                    keys, n = (P, REP) if u == 0 else (SEQ, 2)
                    for h in range(n):
                        r = h if u == 0 else 2 + 2 * u + h
                        a = act.activation(probs[:, u, h * keys:(h + 1) * keys], bank[:, h * keys:(h + 1) * keys],
                                           ACT.Exp, bias=negmax[:, r:r + 1], accum_out=psum_[:, r:r + 1])
                    a.then_inc(s_exp, 1)

                def hi_o():
                    if not real(i, g, 2)[0]:
                        return skip(act, t_hi, i, g, use_o(g), 2)
                    for b in range(NB):
                        split_hi(i, 1 + use_o(g) + b, oT[0][:, b, :, :].rearrange("p h q -> p (h q)"), (use_o(g) + b) % 3)

                new = not isinstance(i, int) or i < NSEQ
                if new:
                    square(0)
                    square(1)
                hi_qk()
                if new:
                    normalise(0)
                    normalise(1)
                hi_probs()
                exps(0)
                exps(1)
                if new:
                    square(2)
                if g == NG - 1:
                    split_hi(i, 1 + use_x(), xT[0][:, :, :].rearrange("p k n -> p (k n)"), xb)
                exps(2)
                if new:
                    normalise(2)
                hi_o()

            run(act, body, begin)

        @block.gpsimd
        def _(pool):
            def begin():
                for s in (rstd_ready, m2_ready, ln_r, var_ready):
                    pool.sem_inc(s, 1)
                pool.memset(half[:, :], -0.5).then_inc(const_made, 1)
                pool.memset(deps[:, :], D * EPS).then_inc(const_made, 1)
                pool.wait_ge(const_made, 2)
                ln_power(0)

            def ln_power(i):
                pool.wait_ge(ln_v, nth(1, i, 1))
                pool.tensor_tensor(ln_rstd[:, :], ln_ve[:, :], half[:, 0:NB], ALU.pow).then_inc(ln_r, 1)

            def body(i, g):
                new = not isinstance(i, int) or i < NSEQ

                def power(u):
                    n = REP if u < 2 else NB
                    pool.wait_ge(sq_ready, nth(UA * NG, i, UA * g + u + 1))
                    pool.tensor_tensor(ve[:, u, 0:n], ssum[:, u, 0:n], deps[:, 0:n], ALU.add).then_inc(var_ready, 1)
                    pool.wait_ge(var_ready, nth(UA * NG, i, UA * g + u + 1))
                    pool.tensor_tensor(rstd[:, u, 0:n], ve[:, u, 0:n], half[:, 0:n], ALU.pow).then_inc(rstd_ready, 1)

                def second(u):
                    pool.wait_ge(qn_ready, nth(UA * NG, i, UA * g + u + 1))
                    pool.wait_ge(rot_ready, nth(UA * NG, i, UA * (g - 1) + u + 1))
                    n = REP if u < 2 else NB
                    q = qn[:, u, 0:n * D].rearrange("p (h s d) -> p h s d", s=2, d=D // 2)
                    o = m2[:, u, 0:n * D].rearrange("p (h s d) -> p h s d", s=2, d=D // 2)
                    if u < 2:
                        b = tabB[:, 0, u:u + 1, :].rearrange("p o (s d) -> p o s d", s=2).broadcast_to([P, n, 2, D // 2])
                    else:
                        b = tabB[:, 1, :, :].rearrange("p b (s d) -> p b s d", s=2)
                    pool.tensor_tensor(o[:, :, ::-1, :], q, b, ALU.mult).then_inc(m2_ready, 1)

                if new:
                    power(0)
                    power(1)
                    if g == 0 and isinstance(i, int):
                        pool.wait_ge(tab, 6)
                    second(0)
                    second(1)
                    power(2)
                    second(2)
                    if g == 2:
                        if more(i):
                            ln_power(i + 1)

            run(pool, body, begin)

        @block.vector
        def _(dve):
            def begin():
                for s in (m1_ready, rot_ready, v_ready, t_split, s_max, r_ready, p_ready, wo_added, ln_s,
                          ln_a, ln_v, ln_x):
                    dve.sem_inc(s, 1)
                ln_stat(0)
                ln_apply(0)
                for n in range(len(pieces)):
                    dve.wait_ge(w_loaded[n % STG], 16 * (n // STG + 1))
                    st = piece_stage(n)
                    if pieces[n][0] == "g":
                        heads = st.rearrange("p (h d) -> p h d", d=D)[:, 0:REP + 1, :]
                        dve.tensor_reduce(csum[:, :], heads, AX.X, ALU.add).then_inc(cent, 1)
                        dve.wait_ge(cent, 2 * n + 1)
                        dve.scalar_tensor_tensor(heads, csum[:, :].unsqueeze(2).broadcast_to([P, REP + 1, D]), -1.0 / D,
                                                 heads, ALU.mult, ALU.add).then_inc(cent, 1)
                    dve.wait_ge(w_hi, n + 1)
                    dve.tensor_tensor(piece_ap(n, 1), st, piece_ap(n, 0).bitcast(F32), ALU.subtract).then_inc(w_free, 1)
                    if n == 2 * NG - 1:
                        split_lo(0, 0, xT[0][:, :, :].rearrange("p k n -> p (k n)"),
                                 xT[1][:, :, :].rearrange("p k n -> p (k n)"), use_x() % 3)
                        tables()

            def tables():
                dve.wait_ge(const_loaded, 9 * 16)
                for w, s in ((0, 1.0), (1, float(D) ** 0.5)):
                    g = gain[:, w:w + 1, :].broadcast_to([P, NB, D])
                    b = bias[:, w:w + 1, :].broadcast_to([P, NB, D])
                    dve.scalar_tensor_tensor(tabA[:, w, :, :], cos[:, :, :], s, g, ALU.mult, ALU.mult).then_inc(tab, 1)
                    dve.scalar_tensor_tensor(tabB[:, w, :, :], sin[:, :, :], s, g, ALU.mult, ALU.mult).then_inc(tab, 1)
                    dve.scalar_tensor_tensor(tabC[:, w, :, :], cos[:, :, :], s * float(D) ** -0.5, b, ALU.mult, ALU.mult).then_inc(tab, 1)
                for w, s in ((0, float(D) ** -0.5), (1, 1.0)):
                    b = bias[:, w:w + 1, :].broadcast_to([P, NB, D])
                    if w:
                        dve.wait_ge(tab, 8)
                    dve.scalar_tensor_tensor(m1[:, 0, 0:NB * D].rearrange("p (b d) -> p b d", b=NB), sin[:, :, :], s, b,
                                             ALU.mult, ALU.mult).then_inc(tab, 1)
                    dve.wait_ge(tab, 7 + 2 * w)
                    for half_ in range(2):
                        lo, hi = half_ * D // 2, (1 - half_) * D // 2
                        c = tabC[:, w, :, lo:lo + D // 2]
                        i_ = dve.tensor_tensor(c, c, m1[:, 0, 0:NB * D].rearrange("p (b d) -> p b d", b=NB)[:, :, hi:hi + D // 2],
                                               ALU.add)
                    i_.then_inc(tab, 1)
                dve.wait_ge(tab, 10)

            def ln_stat(i):
                if isinstance(i, int) and i < 2:
                    dve.wait_ge(x_loaded[i], 16)
                for b in range(NB):
                    xb = x[:, bass.ds(i * NB + b, 1), :].rearrange("p o c -> p (o c)")
                    a = dve.bn_stats(ln_stats[:, b, :], xb)
                a.then_inc(ln_s, 1)
                dve.wait_ge(ln_s, nth(1, i, 1))
                dve.memset(spare[:, :], 0.0)
                for b in range(NB):
                    a = dve.bn_aggr(ln_mv[:, b, :], ln_stats[:, b, :])
                a.then_inc(ln_a, 1)
                dve.wait_ge(ln_a, nth(1, i, 1))
                dve.tensor_scalar(ln_ve[:, :], ln_mv[:, :, 1], EPS, None, ALU.add).then_inc(ln_v, 1)

            def ln_apply(i):
                dve.wait_ge(ln_r, nth(1, i, 1))
                for b in range(NB):
                    xb = x[:, bass.ds(i * NB + b, 1), :].rearrange("p o c -> p (o c)")
                    a = dve.tensor_scalar(xhat[:, b, :], xb, ln_mv[:, b, 0:1], ln_rstd[:, b:b + 1], ALU.subtract, ALU.mult)
                a.then_inc(ln_x, 1)

            def split_lo(i, count, hi, lo, bank, width=BANK):
                dve.wait_ge(t_hi, nth(UT, i, count + 1))
                dve.tensor_tensor(lo, T[bank][:, 0:width], hi.bitcast(F32), ALU.subtract).then_inc(t_split, 1)

            def body(i, g):
                new = not isinstance(i, int) or i < NSEQ

                def first(u):
                    dve.wait_ge(qn_ready, nth(UA * NG, i, UA * g + u + 1))
                    dve.wait_ge(t_ready, nth(UT, i, 1 + use_qk(g) - 8 + u + 1 - (g == 0)))
                    n = REP if u < 2 else NB
                    a = tabA[:, 0, u:u + 1, :].broadcast_to([P, n, D]) if u < 2 else tabA[:, 1, :, :]
                    dve.tensor_tensor(m1[:, u, 0:n * D].rearrange("p (h d) -> p h d", d=D),
                                      qn[:, u, 0:n * D].rearrange("p (h d) -> p h d", d=D), a, ALU.mult).then_inc(m1_ready, 1)

                def rotate(u):
                    dve.wait_ge(m1_ready, nth(UA * NG, i, UA * g + u + 1))
                    dve.wait_ge(m2_ready, nth(UA * NG, i, UA * g + u + 1))
                    n = QC if u < 2 else NB * D
                    dve.tensor_tensor(m1[:, u, 0:n], m1[:, u, 0:n], m2[:, u, 0:n], ALU.add).then_inc(rot_ready, 1)

                def lo_v():
                    dve.wait_ge(v_hi, nth(NG, i, g + 1))
                    kv = A[(UA * g + 2) % 2][:, :].rearrange("p (b s d) -> p b s d", b=NB, s=2)
                    dve.tensor_tensor(v[1][:, g, :, :], kv[:, :, 1, :], v[0][:, g, :, :].bitcast(F32),
                                      ALU.subtract).then_inc(v_ready, 1)

                def lo_qk():
                    if not real(i, g, 1)[0]:
                        return skip(dve, t_split, i, g, use_qk(g), 3)
                    for u in range(3):
                        w = QC if u < 2 else NB * P
                        split_lo(i, 1 + use_qk(g) + u, qT[0][:, u, 0:w], qT[1][:, u, 0:w], (use_qk(g) + u) % 3, w)

                def lo_probs():
                    if not real(i, g, 2)[0]:
                        return skip(dve, t_split, i, g, use_p(g), 3)
                    for u in range(3):
                        split_lo(i, 1 + use_p(g) + u, pT[0][:, u, :, :].rearrange("p h q -> p (h q)"),
                                 pT[1][:, u, :, :].rearrange("p h q -> p (h q)"), (use_p(g) + u) % 3)

                def lo_o():
                    if not real(i, g, 2)[0]:
                        return skip(dve, t_split, i, g, use_o(g), 2)
                    for b in range(NB):
                        split_lo(i, 1 + use_o(g) + b, oT[0][:, b, :, :].rearrange("p h q -> p (h q)"),
                                 oT[1][:, b, :, :].rearrange("p h q -> p (h q)"), (use_o(g) + b) % 3)

                def maxima(u):
                    if not real(i, g, 1)[0]:
                        return
                    dve.wait_ge(s_ready, nth(US * NG, i, US * (g - 1) + u + 1))
                    dve.wait_ge(s_exp, nth(US * NG, i, US * (g - 2) + u + 1))
                    n = REP if u == 0 else 2
                    r = 0 if u == 0 else 2 + 2 * u
                    dve.tensor_reduce(negmax[:, r:r + n], S[(US * (g - 1) + u) % 2][:, :].rearrange("p (h k) -> p h k", h=n),
                                      AX.X, ALU.max, negate=True).then_inc(s_max, 1)

                def norm():
                    if not real(i, g, 2)[0]:
                        return
                    dve.wait_ge(s_exp, nth(US * NG, i, US * (g - 1)))
                    dve.reciprocal(rinv[:, :], psum_[:, :]).then_inc(r_ready, 1)
                    dve.wait_ge(r_ready, nth(NG, i, g - 1))
                    for u in range(3):
                        n = REP if u == 0 else 2
                        r = 0 if u == 0 else 2 + 2 * u
                        pr = probs[:, u, :].rearrange("p (h k) -> p h k", h=n)
                        a = dve.tensor_tensor(pr, pr, rinv[:, r:r + n].unsqueeze(2).broadcast_to([P, n, BANK // n]), ALU.mult)
                    a.then_inc(p_ready, 1)

                norm()
                lo_qk()
                if new:
                    first(0)
                    first(1)
                lo_probs()
                maxima(0)
                maxima(1)
                if new:
                    rotate(0)
                    rotate(1)
                    lo_v()
                if g == NG - 1:
                    split_lo(i, 1 + use_x(), xT[0][:, :, :].rearrange("p k n -> p (k n)"),
                             xT[1][:, :, :].rearrange("p k n -> p (k n)"), use_x() % 3)
                maxima(2)
                if new:
                    first(2)
                lo_o()
                if new:
                    rotate(2)
                if g == 1 and more(i):
                    ln_stat(i + 1)
                if g == 2:
                    if more(i):
                        ln_apply(i + 1)
                    if not isinstance(i, int) or i >= 1:
                        dve.wait_ge(wo_ready, nth(1, i, 0))
                        xb = x[:, bass.ds((i - 1) * NB, NB), :].rearrange("p b c -> p (b c)")
                        dve.tensor_tensor(xb, W[:, :], xb, ALU.add).then_inc(wo_added, 1)

            run(dve, body, begin)


PW = 2 * BANK
NP2 = 13
PP0 = -1e38
LAST = 4
SLOTS = 2 * (NF + 2)
STEPS = SLOTS + 4
LG1, LB1, LG2, LB2, FIRST, MK, MV, MR, CK, CR, NCOL = range(11)


def norm_state(sb, sem, name):
    return {
        "stats": sb(f"{name}_stats", [P, NB, 6]), "mv": sb(f"{name}_mv", [P, NB, 2]), "ve": sb(f"{name}_ve", [P, NB]),
        "rstd": sb(f"{name}_rstd", [P, NB]), "spare": sb(f"{name}_spare", [P, 1]),
        "stats_made": sem(f"{name}_stats_made"), "aggregated": sem(f"{name}_aggregated"),
        "var_ready": sem(f"{name}_var_ready"), "rstd_ready": sem(f"{name}_rstd_ready"), "normed": sem(f"{name}_normed"),
    }


def ffn_state(sb, sem, n, banks):
    state = {
        "acc": banks[0], "G": banks[1:3],  "norm": norm_state(sb, sem, f"f{n}"), "xhat": sb(f"f{n}_xhat", [P, NB, HID]),
        "xT": [sb(f"f{n}_xT_{p}", [P, NK, SEQ], F32R) for p in ("hi", "lo")],
        "h": sb(f"f{n}_h", [P, 2, SEQ]),
        "hs": [sb(f"f{n}_h_{p}", [P, 2, SEQ], F32R) for p in ("hi", "lo")],
    }
    for name in ("x_turned", "x_hi", "x_split", "added", "gate_up", "silu", "h_ready", "h_hi", "h_split", "down"):
        state[name if name not in ("silu", "x_hi", "h_hi") else name + "_ready"] = sem(f"f{n}_{name}")
    return state


def tail(nc, sb, sem, banks, x, ident, w_tail, cols_in):
    wt = [sb(f"wt_{p}", [P, NP2, PW], F32R) for p in ("hi", "lo")]
    flat = [w[:, :, :].rearrange("p a b -> p (a b)") for w in wt]

    def weights(piece, chunks, width, skip=0):
        at = piece * PW + skip
        return [w[:, at:at + chunks * width].rearrange("p (c n) -> p c n", c=chunks) for w in flat]

    w_gate, w_up, w_down = weights(0, NK, FF), weights(2, NK, FF), weights(4, NF, HID)
    w_key, w_val = weights(6, NK, FF), weights(8, NF, HID)
    w_proj = [weights(10, NK, HID), weights(10, NK, HID, BANK), weights(11, NK, HID)]
    w_ob, w_cr = weights(11, NK, HID, BANK), weights(12, NK, HID)

    def ranges(n):
        if n == 11:
            return [(0, BANK, 1.0), (BANK, PW, 0.5)]
        return [(0, BANK if n == 12 else PW, {8: 0.5, 9: 0.5}.get(n, 1.0))]

    cols = sb("cols", [P, NCOL, NK])
    half = sb("half2", [P, NB])
    f1, f2 = ffn_state(sb, sem, 1, banks[0:3]), ffn_state(sb, sem, 2, banks[3:6])
    R = banks[6:8]
    rn = norm_state(sb, sem, "r")
    yh = sb("r_yhat", [P, NB, HID])
    diff = yh[:, :, :]
    hT = sb("r_hT", [P, NK, SEQ + 1])
    mixf = sb("r_mix", [P, 2, NK, SEQ])
    mixs = [[sb(f"r_mix{m}_{p}", [P, NK, SEQ], F32R) for p in ("hi", "lo")] for m in range(3)]
    er = sb("r_e2_rinv", [P, 2, NK, SEQ])
    e2, ri = er[:, 0, :, :], er[:, 1, :, :]
    yt = sb("r_y_th", [P, 2, NB, HID])
    y, th = yt[:, 0, :, :], yt[:, 1, :, :]
    ss = [sb(f"r_s_{p}", [P, NF, SEQ], F32R) for p in ("hi", "lo")]
    stage = [t[:, :, :, :].rearrange("p a b c -> p (a b c)") for t in (mixf, er, yt)]
    ST = len(stage)

    names = ("turned hT diffd mix mix_hi mix_split proj first floored exped recip av wkv rtanh o o_hi o_split oproj "
             "y_added xy_added key s s_hi s_split cr ctanh val u x_added").split()
    (turned, h_ready, diffed, mixed, mix_hi, mix_split, proj, first, floored, exped, recip, av, wkv, rtanh, o_ready, o_hi,
     o_split, oproj, y_added, xy_added, key, s_ready, s_hi, s_split, cr, ctanh, val, u_ready, x_added) = (
        sem(f"r_{n}") for n in names)
    w_loaded = [sem(f"w2_loaded{n}") for n in range(ST)]
    w_hi, w_free, cols_loaded, made, made_h = (sem(n) for n in ("w2_hi", "w2_free", "cols_loaded", "made2", "made_h"))

    USES = {
        "cr": (ctanh, 1, 1, 3), "val": (u_ready, 1, 1, 3), "turn0": (h_ready, 2, 1, 2), "k": (first, 1, 1, 2),
        "v": (av, 1, 1, 2), "r": (rtanh, 1, 1, 2), "out": (y_added, 1, 1, 2), "turn1": (h_ready, 2, 2, 2),
        "key0": (s_ready, 4, 1, 2), "key1": (s_ready, 4, 2, 2), "f1": (f1["x_split"], 1, 1, 0),
        "key2": (s_ready, 4, 3, 2), "f2": (f2["x_split"], 1, 1, 3), "key3": (s_ready, 4, 4, 2),
    }
    ORDER = list(USES)

    def bank_of(use):
        return R[ORDER.index(use) % 2]

    def read_before(i, use):
        n = ORDER.index(use) - 2
        s, per, k, lag = USES[ORDER[n]]
        j = i - lag - (n < 0)
        return s, nth(per, min(j, NSEQ - 1) if isinstance(j, int) else j, k)

    def rows(j, b, n=1):
        return x[:, bass.ds(j * NB + b, n), :].rearrange("p o c -> p (o c)")

    def run(eng, ffn_prep, ffn_block, ffn_end, rwkv):
        def body(i):
            def on(lag):
                return not isinstance(i, int) or 0 <= i - lag < NSEQ

            def r(n):
                if n + SLOTS < STEPS and on(3):
                    rwkv(i, i - 3, n + SLOTS)
                if on(2):
                    rwkv(i, i - 2, n)

            def prep(part):
                if on(0):
                    ffn_prep(i, f1, i, part)
                if on(3):
                    ffn_prep(i, f2, i - 3, part)
            for t in range(NF + 2):
                if on(1):
                    ffn_block(f1, i - 1, t)
                r(2 * t)
                if on(LAST):
                    ffn_block(f2, i - LAST, t)
                if t == 9 and on(3):
                    ffn_prep(i, f2, i - 3, 2)
                r(2 * t + 1)
                if t == 8 and on(0):
                    ffn_prep(i, f1, i, 2)
                if t in (5, 7):
                    prep(t == 7)
            if on(1):
                ffn_end(f1, i - 1)
            if on(LAST):
                ffn_end(f2, i - LAST)
        for i in range(LAST + 1):
            body(i)
        with eng.Fori(LAST + 1, NSEQ) as i:
            body(i)
        for i in range(NSEQ, NSEQ + LAST):
            body(i)

    with nc.Block() as block:
        @block.sync
        def _(sp):
            sp.dma_start(cols[:, :, :], cols_in).then_inc(cols_loaded, 16)
            for n in range(NP2):
                if n >= ST:
                    sp.wait_ge(w_free, n - ST + 1)
                width = ranges(n)[-1][1]
                sp.dma_start(stage[n % ST][:, 0:width], w_tail[:, n, 0:width]).then_inc(w_loaded[n % ST], 16)

        @block.tensor
        def _(pe):
            for s in (turned, proj, oproj, key, cr, val, *(f[n] for f in (f1, f2) for n in ("x_turned", "gate_up", "down"))):
                pe.sem_inc(s, 1)

            def turn(src, bank):
                for k in range(NK):
                    for b in range(NB):
                        mm = pe.transpose(bank[:, (k * NB + b) * P:(k * NB + b + 1) * P],
                                          src[:, b, k * P:(k + 1) * P], ident[:, :])
                return mm

            def ffn_prep(i, f, j, part):
                if part < 2:
                    return
                use = "f1" if f is f1 else "f2"
                pe.wait_ge(f["norm"]["normed"], nth(1, j, 1))
                pe.wait_ge(*read_before(i, use))
                turn(f["xhat"], bank_of(use)).then_inc(f["x_turned"], 1)

            def ffn_block(f, j, t):
                if t < NF:
                    if t == 0:
                        pe.wait_ge(f["x_split"], nth(1, j, 1))
                        if isinstance(j, int) and j == 0 and f is f1:
                            pe.wait_ge(w_free, NP2)
                    pe.wait_ge(f["h_ready"], nth(NF, j, t - 1))
                    bank = f["G"][t % 2]
                    for n, w in enumerate((w_gate, w_up)):
                        for k in range(NK):
                            mm = products(pe, bank[:, n * SEQ:(n + 1) * SEQ], [p[:, k, t * P:(t + 1) * P] for p in w],
                                          [p[:, k, :] for p in f["xT"]], k == 0, k == NK - 1)
                    mm.then_inc(f["gate_up"], 1)
                if t >= 2:
                    d = t - 2
                    if d == 0:
                        pe.wait_ge(f["added"], nth(1, j, 0))
                    pe.wait_ge(f["h_split"], nth(NF, j, d + 1))
                    for b in range(NB):
                        mm = products(pe, f["acc"][:, b * HID:(b + 1) * HID], [p[:, d % 2, b * P:(b + 1) * P] for p in f["hs"]],
                                      [p[:, d, :] for p in w_down], d == 0 and b == 0, d == NF - 1)
                    mm.then_inc(f["down"], 1)

            def ffn_end(f, j):
                pass

            def rwkv(i, j, n):
                if n in (3, 13):
                    c = int(n == 13)
                    pe.wait_ge(rn["normed"], nth(3, j, 2 + c))
                    pe.wait_ge(*read_before(i, f"turn{c}"))
                    turn(yh, bank_of(f"turn{c}")).then_inc(turned, 1)
                if n in (6, 7, 8):
                    m = n - 6
                    pe.wait_ge(mix_split, nth(5, j, m + 1))
                    pe.wait_ge(*read_before(i, "kvr"[m]))
                    o = bank_of("kvr"[m])
                    for c in range(NK):
                        for k in range(NK):
                            mm = products(pe, o[:, c * SEQ:(c + 1) * SEQ], [p[:, k, c * P:(c + 1) * P] for p in w_proj[m]],
                                          [p[:, k, :] for p in mixs[m]], k == 0, k == NK - 1)
                    mm.then_inc(proj, 1)
                if n == 11:
                    pe.wait_ge(o_split, nth(1, j, 1))
                    pe.wait_ge(*read_before(i, "out"))
                    o = bank_of("out")
                    for b in range(NB):
                        for k in range(NK):
                            mm = products(pe, o[:, b * HID:(b + 1) * HID], [p[:, k, b * P:(b + 1) * P] for p in mixs[2]],
                                          [p[:, k, :] for p in w_ob], k == 0, k == NK - 1)
                    mm.then_inc(oproj, 1)
                if 16 <= n <= 19:
                    q = n - 16
                    if q == 0:
                        pe.wait_ge(mix_split, nth(5, j, 4))
                    pe.wait_ge(*read_before(i, f"key{q}"))
                    o = bank_of(f"key{q}")
                    for e in range(2):
                        for k in range(NK):
                            mm = products(pe, o[:, e * SEQ:(e + 1) * SEQ],
                                          [p[:, k, (2 * q + e) * P:(2 * q + e + 1) * P] for p in w_key],
                                          [p[:, k, :] for p in mixs[0]], k == 0, k == NK - 1)
                    mm.then_inc(key, 1)
                if n == 20:
                    pe.wait_ge(mix_split, nth(5, j, 5))
                    pe.wait_ge(*read_before(i, "cr"))
                    o = bank_of("cr")
                    for b in range(NB):
                        for k in range(NK):
                            mm = products(pe, o[:, b * HID:(b + 1) * HID], [p[:, k, b * P:(b + 1) * P] for p in mixs[1]],
                                          [p[:, k, :] for p in w_cr], k == 0, k == NK - 1)
                    mm.then_inc(cr, 1)
                if n in (21, 22):
                    if n == 21:
                        pe.wait_ge(*read_before(i, "val"))
                    o = bank_of("val")
                    for q in (2 * (n - 21), 2 * (n - 21) + 1):
                        pe.wait_ge(s_split, nth(4, j, q + 1))
                        for c in (2 * q, 2 * q + 1):
                            for b in range(NB):
                                mm = products(pe, o[:, b * HID:(b + 1) * HID], [p[:, c, b * P:(b + 1) * P] for p in ss],
                                              [p[:, c, :] for p in w_val], c == 0 and b == 0, c == NF - 1)
                    if n == 22:
                        mm.then_inc(val, 1)

            run(pe, ffn_prep, ffn_block, ffn_end, rwkv)

        @block.scalar
        def _(act):
            for s in (h_ready, mix_hi, first, exped, rtanh, o_hi, s_ready, s_hi, ctanh,
                      *(f[n] for f in (f1, f2) for n in ("x_hi_ready", "silu_ready", "h_hi_ready"))):
                act.sem_inc(s, 1)
            for n in range(NP2):
                act.wait_ge(w_loaded[n % ST], 16 * (n // ST + 1))
                for a, b, scale in ranges(n):
                    i_ = act.activation(wt[0][:, n, a:b], stage[n % ST][:, a:b], ACT.Copy, scale=scale)
                i_.then_inc(w_hi, 1)
            act.wait_ge(cols_loaded, 16)

            def ffn_prep(i, f, j, part):
                if part < 2:
                    return
                act.wait_ge(f["x_turned"], nth(1, j, 1))
                act.wait_ge(f["gate_up"], nth(NF, j, 0))
                act.copy(f["xT"][0][:, :, :].rearrange("p k n -> p (k n)"),
                         bank_of("f1" if f is f1 else "f2")[:, :]).then_inc(f["x_hi_ready"], 1)

            def ffn_block(f, j, t):
                if t < NF:
                    act.wait_ge(f["gate_up"], nth(NF, j, t + 1))
                    act.wait_ge(f["h_split"], nth(NF, j, t - 1))
                    act.activation(f["h"][:, t % 2, :], f["G"][t % 2][:, 0:SEQ], ACT.Silu).then_inc(f["silu_ready"], 1)
                if 1 <= t <= NF:
                    d = t - 1
                    act.wait_ge(f["h_ready"], nth(NF, j, d + 1))
                    act.wait_ge(f["down"], nth(NF, j, d - 1))
                    act.copy(f["hs"][0][:, d % 2, :], f["h"][:, d % 2, :]).then_inc(f["h_hi_ready"], 1)

            def ffn_end(f, j):
                pass

            def rwkv(i, j, n):
                def hi_mix(m):
                    act.wait_ge(mixed, nth(5, j, m + 1))
                    if m == 0:
                        act.wait_ge(key, nth(4, j, 0))
                    if m == 1:
                        act.wait_ge(cr, nth(1, j, 0))
                    if m == 2:
                        act.wait_ge(oproj, nth(1, j, 0))
                    if m > 2:
                        act.wait_ge(proj, nth(3, j, m - 2))
                    dst = mixs[m if m < 3 else m - 3][0]
                    act.copy(dst[:, :, :], mixf[:, m % 2 if m < 3 else m - 3, :, :]).then_inc(mix_hi, 1)

                if n in (3, 13):
                    c = int(n == 13)
                    act.wait_ge(turned, nth(2, j, c + 1))
                    act.wait_ge(mixed, nth(5, j, 3 * c))
                    bank = bank_of(f"turn{c}")
                    for k in range(NK):
                        a = act.activation(hT[:, k, 1:SEQ + 1], bank[:, k * SEQ:(k + 1) * SEQ], ACT.Identity,
                                           scale=cols[:, (LG1, LG2)[c], k:k + 1], bias=cols[:, (LB1, LB2)[c], k:k + 1])
                    a.then_inc(h_ready, 1)
                if n == 5:
                    hi_mix(0)
                    hi_mix(1)
                if n == 6:
                    hi_mix(2)
                if n == 7:
                    act.wait_ge(proj, nth(3, j, 1))
                    act.wait_ge(av, nth(1, j, 0))
                    for c in range(NK):
                        a = act.activation(e2[:, c, :], bank_of("k")[:, c * SEQ:(c + 1) * SEQ], ACT.Identity, scale=1.0,
                                           bias=cols[:, FIRST, c:c + 1])
                    a.then_inc(first, 1)
                if n == 8:
                    act.wait_ge(floored, nth(1, j, 1))
                    act.activation(e2[:, :, :], e2[:, :, :], ACT.Exp).then_inc(exped, 1)
                if n == 9:
                    act.wait_ge(proj, nth(3, j, 3))
                    act.wait_ge(u_ready, nth(1, j, 0))
                    act.activation(th[:, :, :].rearrange("p a b -> p (a b)"), bank_of("r")[:, :], ACT.Tanh,
                                   scale=0.5).then_inc(rtanh, 1)
                if n == 10:
                    act.wait_ge(o_ready, nth(1, j, 1))
                    act.copy(mixs[2][0][:, :, :], mixf[:, 1, :, :]).then_inc(o_hi, 1)
                if n in (15, 16):
                    hi_mix(n - 12)
                if 17 <= n <= 20:
                    q = n - 17
                    act.wait_ge(key, nth(4, j, q + 1))
                    if q < 2:
                        act.wait_ge(mix_split, nth(5, j, 4 + q))
                    else:
                        act.wait_ge(s_split, nth(4, j, q - 1))
                    act.activation(mixf[:, q % 2, :, :].rearrange("p a b -> p (a b)"), bank_of(f"key{q}")[:, :],
                                   ACT.Silu).then_inc(s_ready, 1)
                    if q == 0:
                        act.wait_ge(val, nth(1, j, 0))
                    act.wait_ge(s_ready, nth(4, j, q + 1))
                    act.copy(ss[0][:, 2 * q:2 * q + 2, :], mixf[:, q % 2, :, :]).then_inc(s_hi, 1)
                if n == 21:
                    act.wait_ge(cr, nth(1, j, 1))
                    act.wait_ge(o_ready, nth(1, j, 1))
                    act.activation(th[:, :, :].rearrange("p a b -> p (a b)"), bank_of("cr")[:, :], ACT.Tanh,
                                   scale=0.5).then_inc(ctanh, 1)

            run(act, ffn_prep, ffn_block, ffn_end, rwkv)

        @block.gpsimd
        def _(pool):
            for s in (rn, f1["norm"], f2["norm"]):
                pool.sem_inc(s["rstd_ready"], 1)
            for s in (mix_split, o_split, s_split):
                pool.sem_inc(s, 1)
            pool.memset(half[:, :], -0.5).then_inc(made, 1)
            pool.wait_ge(made, 1)

            def root(s, per, j, n):
                pool.wait_ge(s["var_ready"], nth(per, j, n + 1))
                pool.tensor_tensor(s["rstd"][:, :], s["ve"][:, :], half[:, :], ALU.pow).then_inc(s["rstd_ready"], 1)

            def ffn_prep(i, f, j, part):
                if part == 0:
                    root(f["norm"], 1, j, 0)

            def rwkv(i, j, n):
                def lo_mix(m):
                    pool.wait_ge(mix_hi, nth(5, j, m + 1))
                    s = mixs[m if m < 3 else m - 3]
                    pool.tensor_tensor(s[1][:, :, :], mixf[:, m % 2 if m < 3 else m - 3, :, :], s[0][:, :, :].bitcast(F32),
                                       ALU.subtract).then_inc(mix_split, 1)

                if n in (0, 1, 11):
                    root(rn, 3, j, {0: 0, 1: 1, 11: 2}[n])
                if n == 5:
                    lo_mix(0)
                    lo_mix(1)
                if n == 6:
                    lo_mix(2)
                if n == 10:
                    pool.wait_ge(o_hi, nth(1, j, 1))
                    pool.tensor_tensor(mixs[2][1][:, :, :], mixf[:, 1, :, :], mixs[2][0][:, :, :].bitcast(F32),
                                       ALU.subtract).then_inc(o_split, 1)
                if n in (15, 16):
                    lo_mix(n - 12)
                if 17 <= n <= 20:
                    q = n - 17
                    pool.wait_ge(s_hi, nth(4, j, q + 1))
                    pool.tensor_tensor(ss[1][:, 2 * q:2 * q + 2, :], mixf[:, q % 2, :, :],
                                       ss[0][:, 2 * q:2 * q + 2, :].bitcast(F32), ALU.subtract).then_inc(s_split, 1)

            run(pool, ffn_prep, lambda f, j, t: None, lambda f, j: None, rwkv)

        @block.vector
        def _(dve):
            for s in (diffed, mixed, floored, recip, av, wkv, o_ready, y_added, xy_added, u_ready, x_added,
                      *(f[n] for f in (f1, f2) for n in ("x_split", "added", "h_ready", "h_split")),
                      *(f[n] for f in (rn, f1["norm"], f2["norm"])
                        for n in ("stats_made", "aggregated", "var_ready", "normed"))):
                dve.sem_inc(s, 1)
            for n in range(NP2):
                dve.wait_ge(w_hi, n + 1)
                for a, b, scale in ranges(n):
                    i_ = dve.scalar_tensor_tensor(wt[1][:, n, a:b], stage[n % ST][:, a:b], scale,
                                                  wt[0][:, n, a:b].bitcast(F32), ALU.mult, ALU.subtract)
                i_.then_inc(w_free, 1)
            for k in range(NK):
                a = dve.memset(hT[:, k, 0:1], 0.0)
            a.then_inc(made_h, 1)
            dve.wait_ge(made_h, 1)
            dve.wait_ge(cols_loaded, 16)

            def measure(s, per, j, n, src):
                for b in range(NB):
                    a = dve.bn_stats(s["stats"][:, b, :], src(b))
                a.then_inc(s["stats_made"], 1)
                dve.wait_ge(s["stats_made"], nth(per, j, n + 1))
                dve.memset(s["spare"][:, :], 0.0)
                for b in range(NB):
                    a = dve.bn_aggr(s["mv"][:, b, :], s["stats"][:, b, :])
                a.then_inc(s["aggregated"], 1)
                dve.wait_ge(s["aggregated"], nth(per, j, n + 1))
                dve.tensor_scalar(s["ve"][:, :], s["mv"][:, :, 1], EPS, None, ALU.add).then_inc(s["var_ready"], 1)

            def apply(s, per, j, n, src, dst):
                dve.wait_ge(s["rstd_ready"], nth(per, j, n + 1))
                for b in range(NB):
                    a = dve.tensor_scalar(dst(b), src(b), s["mv"][:, b, 0:1], s["rstd"][:, b:b + 1], ALU.subtract,
                                          ALU.mult)
                a.then_inc(s["normed"], 1)

            def ffn_prep(i, f, j, part):
                if part == 0:
                    if f is f2:
                        dve.wait_ge(x_added, nth(1, j, 1))
                        dve.memset(f["norm"]["spare"][:, :], 0.0)
                    measure(f["norm"], 1, j, 0, lambda b: rows(j, b))
                if part == 1:
                    dve.wait_ge(f["x_turned"], nth(1, j, 0))
                    apply(f["norm"], 1, j, 0, lambda b: rows(j, b), lambda b: f["xhat"][:, b, :])
                if part == 2:
                    dve.wait_ge(f["x_hi_ready"], nth(1, j, 1))
                    dve.tensor_tensor(f["xT"][1][:, :, :].rearrange("p k n -> p (k n)"),
                                      bank_of("f1" if f is f1 else "f2")[:, :],
                                      f["xT"][0][:, :, :].rearrange("p k n -> p (k n)").bitcast(F32),
                                      ALU.subtract).then_inc(f["x_split"], 1)

            def ffn_block(f, j, t):
                if t < NF:
                    dve.wait_ge(f["silu_ready"], nth(NF, j, t + 1))
                    h = f["h"][:, t % 2, :]
                    dve.tensor_tensor(h, h, f["G"][t % 2][:, SEQ:2 * SEQ], ALU.mult).then_inc(f["h_ready"], 1)
                if 1 <= t <= NF:
                    d = t - 1
                    dve.wait_ge(f["h_hi_ready"], nth(NF, j, d + 1))
                    dve.tensor_tensor(f["hs"][1][:, d % 2, :], f["h"][:, d % 2, :], f["hs"][0][:, d % 2, :].bitcast(F32),
                                      ALU.subtract).then_inc(f["h_split"], 1)

            def ffn_end(f, j):
                dve.wait_ge(f["down"], nth(NF, j, NF))
                dve.tensor_tensor(rows(j, 0, NB), f["acc"][:, :], rows(j, 0, NB), ALU.add).then_inc(f["added"], 1)

            def rwkv(i, j, n):
                def mix(m, row):
                    s, per, k = [(x_added, 1, 0), (s_split, 4, 0), (mix_split, 5, 1), (mix_split, 5, 3), (o_split, 1, 1)][m]
                    dve.wait_ge(s, nth(per, j, k))
                    for k in range(NK):
                        a = dve.scalar_tensor_tensor(mixf[:, m % 2 if m < 3 else m - 3, k, :], diff[:, k, :],
                                                     cols[:, row, k:k + 1], hT[:, k, 0:SEQ], ALU.mult, ALU.add)
                    a.then_inc(mixed, 1)

                def difference(c):
                    dve.wait_ge(h_ready, nth(2, j, c + 1))
                    dve.tensor_tensor(diff, hT[:, :, 1:SEQ + 1], hT[:, :, 0:SEQ], ALU.subtract).then_inc(diffed, 1)
                    dve.wait_ge(diffed, nth(2, j, c + 1))

                if n == 0:
                    dve.wait_ge(f1["added"], nth(1, j, 1))
                    dve.memset(rn["spare"][:, :], 0.0)
                    measure(rn, 3, j, 0, lambda b: rows(j, b))
                if n == 1:
                    apply(rn, 3, j, 0, lambda b: rows(j, b), lambda b: y[:, b, :])
                    dve.wait_ge(rn["normed"], nth(3, j, 1))
                    measure(rn, 3, j, 1, lambda b: y[:, b, :])
                if n == 2:
                    dve.wait_ge(turned, nth(2, j, 0))
                    dve.wait_ge(mixed, nth(5, j, 0))
                    apply(rn, 3, j, 1, lambda b: y[:, b, :], lambda b: yh[:, b, :])
                if n == 4:
                    difference(0)
                    mix(0, MK)
                    mix(1, MV)
                if n == 6:
                    mix(2, MR)
                if n == 7:
                    dve.wait_ge(first, nth(1, j, 1))
                    dve.tensor_scalar(e2[:, :, :], e2[:, :, :], PP0, 0.0, ALU.subtract, ALU.min).then_inc(floored, 1)
                if n == 8:
                    dve.wait_ge(exped, nth(1, j, 1))
                    dve.reciprocal(ri[:, :, :], e2[:, :, :]).then_inc(recip, 1)
                    dve.wait_ge(proj, nth(3, j, 2))
                    dve.wait_ge(recip, nth(1, j, 1))
                    dve.tensor_tensor(e2[:, :, :].rearrange("p a b -> p (a b)"), bank_of("v")[:, :],
                                      e2[:, :, :].rearrange("p a b -> p (a b)"), ALU.mult).then_inc(av, 1)
                    dve.wait_ge(av, nth(1, j, 1))
                    dve.tensor_tensor(ri[:, :, :], e2[:, :, :], ri[:, :, :], ALU.mult).then_inc(wkv, 1)
                if n == 9:
                    dve.wait_ge(rtanh, nth(1, j, 1))
                    dve.wait_ge(wkv, nth(1, j, 1))
                    dve.wait_ge(mix_split, nth(5, j, 2))
                    dve.scalar_tensor_tensor(mixf[:, 1, :, :], th[:, :, :], 1.0, ri[:, :, :], ALU.add,
                                             ALU.mult).then_inc(o_ready, 1)
                if n == 11:
                    dve.wait_ge(oproj, nth(1, j, 1))
                    yf = y[:, :, :].rearrange("p b c -> p (b c)")
                    dve.tensor_tensor(yf, bank_of("out")[:, :], yf, ALU.add).then_inc(y_added, 1)
                    dve.wait_ge(y_added, nth(1, j, 1))
                    measure(rn, 3, j, 2, lambda b: y[:, b, :])
                if n == 12:
                    dve.wait_ge(mixed, nth(5, j, 3))
                    apply(rn, 3, j, 2, lambda b: y[:, b, :], lambda b: yh[:, b, :])
                    yf = y[:, :, :].rearrange("p b c -> p (b c)")
                    dve.tensor_tensor(rows(j, 0, NB), yf, rows(j, 0, NB), ALU.add).then_inc(xy_added, 1)
                if n == 14:
                    difference(1)
                    mix(3, CK)
                if n == 15:
                    mix(4, CR)
                if n == 23:
                    dve.wait_ge(ctanh, nth(1, j, 1))
                    dve.wait_ge(val, nth(1, j, 1))
                    dve.wait_ge(s_split, nth(4, j, 3))
                    dve.scalar_tensor_tensor(mixf[:, 0, :, :].rearrange("p a b -> p (a b)"),
                                             th[:, :, :].rearrange("p a b -> p (a b)"), 1.0, bank_of("val")[:, :], ALU.add,
                                             ALU.mult).then_inc(u_ready, 1)
                    dve.wait_ge(u_ready, nth(1, j, 1))
                    dve.tensor_tensor(rows(j, 0, NB), mixf[:, 0, :, :].rearrange("p a b -> p (a b)"), rows(j, 0, NB),
                                      ALU.add).then_inc(x_added, 1)

            run(dve, ffn_prep, ffn_block, ffn_end, rwkv)


_INS = ["x_in", "w_group", "w_out", "qg", "qb", "kg", "kb", "cos_t", "sin_t", "ident_in", "identb_in", "mask_in",
        "w_tail", "cols_in"]


def kernel(**inp):
    import ml_dtypes
    import numpy as np
    import concourse.bacc as bacc
    from concourse import mybir as mb
    from concourse.bass_utils import run_bass_kernel_spmd

    a = {k: np.asarray(v) for k, v in inp.items()}
    wqkv = a["L0_attn_a_w_qkv"]
    q, k, v = wqkv[:HEADS * D], wqkv[HEADS * D:(HEADS + KV) * D], wqkv[(HEADS + KV) * D:]
    grouped = np.concatenate([q.reshape(NG, QC, HID), k.reshape(NG, D, HID), v.reshape(NG, D, HID)], 1)
    w_group = grouped.reshape(NG, GW, NK, P).transpose(2, 0, 3, 1)
    w_out = a["L0_attn_a_w_o"].reshape(HID, HEADS, D).transpose(2, 1, 0)
    freq = (1.0 / np.float32(1000000.0) ** (np.arange(0, D, 2, dtype=np.float32) / np.float32(D))).astype(np.float32)
    ang = np.outer(np.arange(SEQ, dtype=np.float32), freq).astype(np.float32)
    cos, sin = np.cos(ang), np.sin(ang)
    tri = np.where(np.arange(P)[None, :] > np.arange(P)[:, None], np.float32(MASKED), np.float32(0.0))
    def turned(name, chunks):
        w = a[name]
        return w.T.reshape(chunks, P, w.shape[0]).transpose(1, 0, 2).reshape(P, -1)

    b = "L0_attn_b_"
    w_tail = np.concatenate([turned("L0_ffn_w_gate", NK), turned("L0_ffn_w_up", NK), turned("L0_ffn_w_down", NF),
                             turned(b + "Wkey", NK), turned(b + "Wval", NF), turned(b + "Wk", NK), turned(b + "Wv", NK),
                             turned(b + "Wr", NK), turned(b + "Wo", NK), turned(b + "Wcr", NK),
                             np.zeros((P, BANK), np.float32)], 1).reshape(P, NP2, PW)
    cols_in = np.stack([a[b + n].reshape(NK, P).T for n in
                        ("ln1_g", "ln1_b", "ln2_g", "ln2_b", "tm_first", "tm_mk", "tm_mv", "tm_mr", "cm_mk", "cm_mr")], 1)
    arrays = {
        "w_tail": w_tail, "cols_in": cols_in,
        "x_in": a["L0_attn_a_x"], "w_group": w_group, "w_out": w_out,
        "qg": a["L0_attn_a_qn_g"], "qb": a["L0_attn_a_qn_b"], "kg": a["L0_attn_a_kn_g"], "kb": a["L0_attn_a_kn_b"],
        "cos_t": np.concatenate([cos, cos], 1), "sin_t": np.concatenate([sin, -sin], 1),
        "ident_in": np.eye(P, dtype=np.float32), "identb_in": np.eye(P, dtype=ml_dtypes.bfloat16),
        "mask_in": tri.astype(ml_dtypes.bfloat16),
    }
    nc = bacc.Bacc("TRN2", target_bir_lowering=False, num_devices=1)
    arrays = {n: np.ascontiguousarray(arrays[n]) for n in _INS}
    aps = [nc.dram_tensor(n, arrays[n].shape, mb.dt.from_np(arrays[n].dtype), kind="ExternalInput").ap() for n in _INS]
    out = nc.dram_tensor("out", (NSEQ, SEQ, HID), mb.dt.float32, kind="ExternalOutput").ap()
    kernel_program(nc, *aps, out)
    r = run_bass_kernel_spmd(nc, [arrays], core_ids=[0])
    return r.results[0]["out"]
```
